# Optimizing a Trainium2 kernel written in Bass

```python
import numpy as np
import jax
import jax.numpy as jnp

def _softmax(x, axis=-1):
    return jax.nn.softmax(x, axis=axis)

def _gelu(x):
    return jax.nn.gelu(x, approximate=True)

def _silu(x):
    return jax.nn.silu(x)

def _sigmoid(x):
    return jax.nn.sigmoid(x)

def _layernorm(x, axis=-1, eps=1e-05):
    m = jnp.mean(x, axis=axis, keepdims=True)
    v = jnp.var(x, axis=axis, keepdims=True)
    return (x - m) / jnp.sqrt(v + eps)

def _scatter_add(tgt, idx, src, axis=0):
    return tgt.at[idx].add(src)

def _segment_sum(src, seg, n):
    return jax.ops.segment_sum(src, seg, n)
kernel_name = 'mk_gnn_preln_d1_gnn_r8_cac31f'

def setup_inputs(seed: int=0):
    np.random.seed(seed)
    _w = jnp.asarray

    def _rec_inputs():
        import jax
        import jax.numpy as jnp
        _gk = jax.random.key(seed)
        x = -0.0003713 + 1 * jax.random.normal(jax.random.fold_in(_gk, 1), (6250, 128), jnp.float32)
        _s = jax.random.randint(jax.random.fold_in(_gk, 2), (50000,), 0, 6250, jnp.int32)
        _d = jax.random.randint(jax.random.fold_in(_gk, 3), (50000,), 0, 6250, jnp.int32)
        _loop = jnp.arange(6250, dtype=jnp.int32)
        src = jnp.concatenate([_s, _d, _loop])
        dst = jnp.concatenate([_d, _s, _loop])
        _o = jnp.argsort(dst, stable=True)
        src = src[_o]
        dst = dst[_o]
        edge_type_8 = jax.random.randint(jax.random.fold_in(_gk, 12), (106250,), 0, 8, jnp.int32)
        return (x, src, dst, edge_type_8)
    x, src, dst, edge_type_8 = _rec_inputs()

    def _L0_gnn_setup():
        import jax, jax.numpy as jnp
        import numpy as np
        N_NODES = 12500
        N_EDGES = 75000
        DIM = 128
        NUM_RELS = 8
        key = jax.random.key(seed)
        k_x, k_ei, k_et, k_w, k_root = jax.random.split(key, 5)
        x = jax.random.normal(k_x, (N_NODES, DIM), dtype=jnp.float32)
        edge_index = jax.random.randint(k_ei, (2, N_EDGES), 0, N_NODES, dtype=jnp.int64)
        edge_type = jax.random.randint(k_et, (N_EDGES,), 0, NUM_RELS, dtype=jnp.int64)
        W = jax.random.normal(k_w, (NUM_RELS, DIM, DIM), dtype=jnp.float32) * 0.05
        W_root = jax.random.normal(k_root, (DIM, DIM), dtype=jnp.float32) * 0.05
        bias = jnp.zeros((DIM,), dtype=jnp.float32)
        return {'x': x, 'W': W, 'W_root': W_root, 'bias': bias, 'edge_index': edge_index, 'edge_type': edge_type}
    _L0_gnn_all = _L0_gnn_setup()
    _L0_gnn_in = {k: v for k, v in _L0_gnn_all.items() if k in ('W', 'W_root', 'bias')}
    del _L0_gnn_all
    return {'x': x, 'src': src, 'dst': dst, 'edge_type_8': edge_type_8, 'L0_gnn_W': _L0_gnn_in['W'], 'L0_gnn_W_root': _L0_gnn_in['W_root'], 'L0_gnn_bias': _L0_gnn_in['bias']}

def reference(x, src, dst, edge_type_8, L0_gnn_W, L0_gnn_W_root, L0_gnn_bias):
    import jax
    import jax.numpy as jnp

    def _L0_gnn_ref(x, W, W_root, bias, edge_index, edge_type):
        import jax, jax.numpy as jnp
        import numpy as np
        N_NODES = 12500
        N_EDGES = 75000
        DIM = 128
        NUM_RELS = 8
        "RGCNConv (num_bases=None, aggr='mean'):\n            out[i] = x[i] @ W_root + bias + sum_r mean_{j in N_r(i)} (x[j] @ W[r])\n            "
        src = edge_index[0]
        dst = edge_index[1]
        n = x.shape[0]
        num_rels = W.shape[0]
        x_j = x[src]
        out = x @ W_root + bias
        for r in range(num_rels):
            m = (edge_type == r).astype(x.dtype)
            msg = x_j @ W[r] * m[:, None]
            agg = jax.ops.segment_sum(msg, dst, num_segments=n)
            cnt = jax.ops.segment_sum(m, dst, num_segments=n)
            out = out + agg / jnp.maximum(cnt, 1.0)[:, None]
        return out
    edge_index = jnp.stack([src, dst])
    h = jnp.maximum(_layernorm(x, axis=-1), 0.0)
    x = x + _L0_gnn_ref(h, L0_gnn_W, L0_gnn_W_root, L0_gnn_bias, edge_index, edge_type_8)
    return x

_drawn_inputs = setup_inputs


def setup_inputs(seed=0):
    import zlib

    import numpy as np

    out = dict(_drawn_inputs(seed))
    spreads = {'L0_gnn_bias': (0.0, 0.1)}
    factors = {}
    for name, (base, spread) in spreads.items():
        noise = np.random.default_rng([zlib.crc32(name.encode()), seed]).standard_normal(out[name].shape)
        drawn = base * np.exp(spread * noise) if base else spread * noise
        out[name] = jnp.asarray(drawn.astype(out[name].dtype))
    for name, factor in factors.items():
        out[name] = (out[name] * factor).astype(out[name].dtype)
    return out
```

```python
from contextlib import ExitStack
from math import ceil, floor, sqrt

import numpy as np

import concourse.bass as bass
from concourse import mybir

P = 128
F = 128
R = 8
N = 6250
E = 106250
TILES = ceil(E / P)
GT = 3
GROUPS = 5
IT = GT * GROUPS
BLK = 112
ITERS = ceil(TILES / IT)
BLOCKS = ceil(N / BLK)
LAG = 2
GALL = ceil(TILES / GT)
LASTN = N - (BLOCKS - 1) * BLK
RING = 5
LIVE = 4
SEG = BLK * R
CHUNKS = ceil(TILES / P)
ROWS_L = TILES - (CHUNKS - 1) * P
EDGES_L = E - (TILES - 1) * P
PAD_DST = -1
EPS = 1e-5
NODES_PER_TILE = N * P / E
FLAT = 6.0


def window(j):
    a, b = j * NODES_PER_TILE, (j + 1) * NODES_PER_TILE
    spread = lambda nodes: FLAT * sqrt(nodes * N / E)
    return max(0, floor(a - spread(a))), ceil(b + 1 + spread(b))


WINDOWS = [window(j) for j in range(GT)]
WIN = WINDOWS[-1][1] * R
OHW = max(b - a for a, b in WINDOWS) * R
SPAN = RING * BLK * R
TRASH = BLOCKS * SEG
OWN_AT = 3
INV_STEPS = 5
PARTS = 3
CHECKS = 2 * GT + 4
VW = F + 4
assert 2 * WIN <= 512 and BLOCKS == ITERS and GALL * GT == TILES


def rgcn(nc, x, src, dst, etype, w, w_root, bias, out):
    f32, bf16, i32 = mybir.dt.float32, mybir.dt.bfloat16, mybir.dt.int32
    ALU, ACT, AX = mybir.AluOpType, mybir.ActivationFunctionType, mybir.AxisListType
    sums = nc.dram_tensor("segment_sums", [TRASH + P, VW], f32, kind="Internal").ap()

    with ExitStack() as ctx:
        def sb(name, shape, dt=f32):
            return ctx.enter_context(nc.sbuf_tensor(name, shape, dt))

        def pb(name, shape, dt=f32):
            return ctx.enter_context(nc.psum_tensor(name, shape, dt))

        def sem(name):
            return ctx.enter_context(nc.semaphore(name))

        e_rows_i = sb("e_rows_i", [P, 3, CHUNKS, P], i32)
        e_rows = sb("e_rows", [P, 3, CHUNKS, P])
        src_i = sb("src_i", [P, CHUNKS * P], i32)
        dst_f = sb("dst_f", [P, CHUNKS * P])
        type_f = sb("type_f", [P, CHUNKS * P])
        seg_f = sb("seg_f", [P, CHUNKS * P])
        rel_f = sb("rel_f", [P, GALL * GT])
        base8 = sb("base8", [P, GALL])
        base_i = sb("base_i", [1, GALL], i32)
        idx = sb("idx", [P, IT], i32)
        xg = sb("xg", [P, IT, F])
        hg = sb("hg", [P, IT, F])
        onehot = sb("onehot", [P, IT, OHW])
        stats = sb("stats", [P, GROUPS, GT + 1, 6])
        mv = sb("mv", [P, GROUPS, GT + 1, 2])
        std = sb("std", [P, GROUPS, GT + 1])
        rstd = sb("rstd", [P, GROUPS, GT + 1])
        nmr = sb("nmr", [P, GROUPS, GT + 1])
        ring = sb("ring", [P, 2, SPAN + WIN])
        means = sb("means", [P, R, BLK])
        x_own = sb("x_own", [P, F])
        h_own = sb("h_own", [P, F])
        hT = sb("hT", [P, BLK])
        cnt_row = sb("cnt_row", [1, SEG])
        inv = sb("inv", [BLK, R])
        rest = sb("rest", [BLK, R])
        inv_parts = sb("inv_parts", [BLK, PARTS, R], bf16)
        invT = sb("invT", [PARTS * R, BLK], bf16)
        pick = sb("pick", [PARTS * R, R, P], bf16)
        y = sb("y", [P, F])
        w_sb = sb("w_sb", [P, R, F])
        wr_sb = sb("wr_sb", [P, F])
        bias_sb = sb("bias_sb", [1, F])
        ident = sb("ident", [P, P])
        ident_bf = sb("ident_bf", [P, P], bf16)
        first = sb("first", [P, P])
        ones = sb("ones", [P, P])
        ones_bf = sb("ones_bf", [P, P], bf16)
        iota = sb("iota", [P, WIN])
        zeros = sb("zeros", [P, SEG])
        eps = sb("eps", [P, 1])
        lin8 = sb("lin8", [P, ITERS * GROUPS])
        dev8 = sb("dev8", [P, GALL])
        ext = sb("ext", [P, CHECKS])
        bad = sb("bad", [P, CHECKS])
        bad1 = sb("bad1", [P, 1])
        flag = sb("flag", [1, 1], i32)
        g_idx = sb("g_idx", [P, 1], i32)
        g_put = sb("g_put", [P, 1], i32)
        g_x = sb("g_x", [P, F])
        g_h = sb("g_h", [P, VW])
        g_v = sb("g_v", [P, VW])
        g_key = sb("g_key", [P, P])
        g_eq = sb("g_eq", [P, P])
        g_low = sb("g_low", [P, P])
        g_tmp = sb("g_tmp", [P, P])
        g_col = sb("g_col", [P, 8])
        g_row = sb("g_row", [P, 1])
        g_s = sb("g_s", [P, R, VW])
        g_c = sb("g_c", [P, R])

        acc = pb("acc", [P, GROUPS, 2, 256])
        fin = pb("fin", [P, 2, 512])
        zp = pb("zp", [P, 512])
        finT = fin[:, 0, :].bitcast(bf16)

        src0_in, consts_in = sem("src0_in"), sem("consts_in")
        edges_in = [sem("src_in"), sem("dst_in"), sem("type_in")]
        pads, ident_made, pick_made = sem("pads"), sem("ident_made"), sem("pick_made")
        iota_made, low_made = sem("iota_made"), sem("low_made")
        filled, first_zero = sem("filled"), sem("first_zero")
        table_loaded = sem("table_loaded")
        src0_f, dst_conv, type_conv, srcs_conv = sem("src0_f"), sem("dst_conv"), sem("type_conv"), sem("srcs_conv")
        src0_T, dst_T, type_T, srcs_T, base_T = sem("src0_T"), sem("dst_T"), sem("type_T"), sem("srcs_T"), sem("base_T")
        src0_i, srcs_i, type_sb, dst_sb = sem("src0_i"), sem("srcs_i"), sem("type_sb"), sem("dst_sb")
        seg_ready, base_ready, rel_ready = sem("seg_ready"), sem("base_ready"), sem("rel_ready")
        idx_ready = sem("idx_ready")
        gathered = [sem(f"gathered{j}") for j in range(IT)]
        passed = sem("passed")
        stats_done, aggr_done = sem("stats_done"), sem("aggr_done")
        std_ready, rstd_done, norm_ready = sem("std_ready"), sem("rstd_done"), sem("norm_ready")
        h_ready, onehot_ready = sem("h_ready"), sem("onehot_ready")
        group_summed, group_added = sem("group_summed"), sem("group_added")
        own_in, own_h, own_T, own_sb = sem("own_in"), sem("own_h"), sem("own_T"), sem("own_sb")
        fold_done, summed, slot_clear = sem("fold_done"), sem("summed"), sem("slot_clear")
        cnt_sb, cnt_T, inv_step, inv_ready = sem("cnt_sb"), sem("cnt_T"), sem("inv_step"), sem("inv_ready")
        inv_T, inv_sb, inv_spread = sem("inv_T"), sem("inv_sb"), sem("inv_spread")
        means_ready, z_done, y_ready, stored = sem("means_ready"), sem("z_done"), sem("y_ready"), sem("stored")
        check_step, bad_ready, bad_sum, flag_ready = sem("check_step"), sem("bad_ready"), sem("bad_sum"), sem("flag_ready")
        g_added, g_step, g_const = sem("g_added"), sem("g_step"), sem("g_const")
        g_idx_ready, g_gathered, g_var, g_std = sem("g_idx_ready"), sem("g_gathered"), sem("g_var"), sem("g_std")
        g_norm, g_h_ready, g_keys, g_spread = sem("g_norm"), sem("g_h_ready"), sem("g_keys"), sem("g_spread")
        g_eq_ready, g_summed, g_put_ready, g_put_written = (
            sem("g_eq_ready"), sem("g_summed"), sem("g_put_ready"), sem("g_put_written"))
        g_in, g_sums_in, g_means, g_T = sem("g_in"), sem("g_sums_in"), sem("g_means"), sem("g_T")
        g_own_T, g_own_sb, g_means_sb, g_z, g_y, g_stored = (
            sem("g_own_T"), sem("g_own_sb"), sem("g_means_sb"), sem("g_z"), sem("g_y"), sem("g_stored"))

        block = ctx.enter_context(nc.Block())

        def static(i, value=0):
            return isinstance(i, int) and i == value

        def tiles_in(i, q):
            return GT if not isinstance(i, int) else max(0, min(GT, TILES - i * IT - q * GT))

        def block_of(i, lag=LAG):
            return None if isinstance(i, int) and i < lag else i - lag

        def rows_of(b):
            return LASTN if static(b, BLOCKS - 1) else BLK

        def settled(eng):
            eng.sem_inc(passed, 1)

        def run_iterations(eng, iteration):
            for i in range(LAG + 2):
                iteration(i)
            with eng.Fori(LAG + 2, ITERS - 1) as i:
                iteration(i)
            iteration(ITERS - 1)

        acc_flat = acc[:, :, :, :].rearrange("p q a w -> p (q a w)")
        dstT = acc_flat[:, 0:CHUNKS * P]
        typeT = acc_flat[:, 1024:1024 + CHUNKS * P]
        baseT = acc_flat[:, 2048:2048 + GALL]
        fin_flat = fin[:, :, :].rearrange("p a w -> p (a w)")
        srcT = fin_flat[:, 0:(CHUNKS - 1) * P]

        @block.sync
        def _(sp):
            def chunk0(a, v, s):
                sp.dma_start(e_rows_i[:, a, 0, :], v[0:P * P].rearrange("(t e) -> t e", e=P)).then_inc(s, 16)

            chunk0(0, src, src0_in)
            for a, v in ((1, dst), (2, etype), (0, src)):
                if a:
                    chunk0(a, v, edges_in[a])
                sp.dma_start(e_rows_i[:, a, 1:CHUNKS - 1, :], v[P * P:(CHUNKS - 1) * P * P]
                             .rearrange("(c t e) -> t c e", t=P, e=P)).then_inc(edges_in[a], 16)
                sp.wait_ge(pads, 3)
                sp.dma_start(e_rows_i[0:ROWS_L - 1, a, CHUNKS - 1, :],
                             v[(CHUNKS - 1) * P * P:(TILES - 1) * P].rearrange("(t e) -> t e", e=P)).then_inc(edges_in[a], 16)
                sp.dma_start(e_rows_i[ROWS_L - 1:ROWS_L, a, CHUNKS - 1, 0:EDGES_L],
                             v[(TILES - 1) * P:E].rearrange("(t e) -> t e", t=1)).then_inc(edges_in[a], 16)
            sp.dma_start(w_sb[:, :, :], w.rearrange("r k n -> k r n")).then_inc(consts_in, 16)
            sp.dma_start(wr_sb[:, :], w_root).then_inc(consts_in, 16)
            sp.dma_start(bias_sb[:, :], bias.rearrange("(a n) -> a n", a=1)).then_inc(consts_in, 16)
            sp.dma_start(x_own[0:BLK, :], x[0:BLK, :]).then_inc(own_in, 16)

            def store(b, n):
                sp.wait_ge(y_ready, b + 1)
                sp.dma_start(out[bass.ds(b * BLK, n), :], y[0:n, :]).then_inc(stored, 16)

            def load(b, n):
                sp.dma_start(x_own[0:n, :], x[bass.ds(b * BLK, n), :]).then_inc(own_in, 16)

            with sp.Fori(0, BLOCKS - 2) as b:
                store(b, BLK)
                load(b + 1, BLK)
            store(BLOCKS - 2, BLK)
            load(BLOCKS - 1, LASTN)
            store(BLOCKS - 1, LASTN)
            sp.wait_ge(stored, 16 * BLOCKS)

            sp.wait_ge(flag_ready, 1)
            general = sp.value_load(flag[0:1, 0:1], min_val=0, max_val=1)
            with sp.If(general):
                sp.dma_start(sums.rearrange("(p a) c -> p a c", p=P),
                             zeros[:, 0:VW].unsqueeze(1).to_broadcast([P, (TRASH + P) // P, VW])).then_inc(g_added, 16)
                sp.wait_ge(g_added, 16 * (1 + TILES))

                def block_io(b, n, before):
                    if before is not None:
                        sp.wait_ge(g_stored, before)
                    sp.dma_start(g_s[0:n, :, :], sums[bass.ds(b * SEG, n * R), :]
                                 .rearrange("(n r) c -> n r c", r=R)).then_inc(g_sums_in, 16)
                    sp.dma_start(x_own[0:n, :], x[bass.ds(b * BLK, n), :]).then_inc(g_in, 16)
                    sp.wait_ge(g_y, b + 1)
                    sp.dma_start(out[bass.ds(b * BLK, n), :], y[0:n, :]).then_inc(g_stored, 16)

                block_io(0, BLK, None)
                with sp.Fori(1, BLOCKS - 1) as b:
                    block_io(b, BLK, 16 * b)
                block_io(BLOCKS - 1, LASTN, 16 * (BLOCKS - 1))
                sp.wait_ge(g_stored, 16 * BLOCKS)
                settled(sp)

        @block.gpsimd
        def _(pool):
            for a, v in ((0, 0), (1, PAD_DST), (2, 0)):
                nc.gpsimd.memset(e_rows_i[:, a, CHUNKS - 1, :], v).then_inc(pads, 1)
            nc.gpsimd.memset(ident[:, :], 0.0).then_inc(ident_made, 1)
            pool.wait_ge(ident_made, 1)
            nc.gpsimd.affine_select(out=ident[:, :], in_=ident[:, :], compare_op=ALU.not_equal, fill=1.0,
                                    base=0, pattern=[[-1, P]], channel_multiplier=1).then_inc(ident_made, 1)
            nc.gpsimd.iota(iota[:, :], [[1, WIN]], base=0, channel_multiplier=0,
                           allow_small_or_imprecise_dtypes=True).then_inc(iota_made, 1)

            def gathers(i, n):
                for j in range(n):
                    if j % GT == 0:
                        pool.wait_ge(idx_ready, i * GROUPS + j // GT + 1)
                        settled(pool)
                    nc.gpsimd.indirect_dma_start(
                        out=xg[:, j, :], out_offset=None, in_=x,
                        in_offset=bass.IndirectOffsetOnAxis(ap=idx[:, j:j + 1], axis=0)).then_inc(gathered[j], 16)
                    if static(i) and j == GT - 1:
                        nc.gpsimd.tensor_copy(ident_bf[:, :], ident[:, :]).then_inc(ident_made, 1)
                        nc.gpsimd.memset(pick[:, :, :], 0.0).then_inc(pick_made, 1)
                        for k in range(PARTS):
                            pool.wait_ge(pick_made, k + 1)
                            nc.gpsimd.affine_select(out=pick[:, :, :], in_=pick[:, :, :], compare_op=ALU.not_equal,
                                                    fill=1.0, base=-k * R, pattern=[[-1, R], [0, P]],
                                                    channel_multiplier=1).then_inc(pick_made, 1)
                        nc.gpsimd.iota(lin8[:, :], [[SEG, ITERS], [0, GROUPS]], base=-SEG, channel_multiplier=0,
                                       allow_small_or_imprecise_dtypes=True).then_inc(low_made, 1)

            gathers(0, IT)
            with pool.Fori(1, ITERS - 1) as i:
                gathers(i, IT)
            gathers(ITERS - 1, TILES - (ITERS - 1) * IT)

            pool.wait_ge(flag_ready, 1)
            general = pool.value_load(flag[0:1, 0:1], min_val=0, max_val=1)
            with pool.If(general):
                nc.gpsimd.memset(g_low[:, :], 1.0).then_inc(g_const, 1)
                pool.wait_ge(g_const, 1)
                nc.gpsimd.affine_select(out=g_low[:, :], in_=g_low[:, :], compare_op=ALU.is_gt, fill=0.0,
                                        base=0, pattern=[[-1, P]], channel_multiplier=1).then_inc(g_const, 1)
                nc.gpsimd.iota(g_row[:, :], [[1, 1]], base=TRASH, channel_multiplier=1,
                               allow_small_or_imprecise_dtypes=True).then_inc(g_const, 1)
                with pool.Fori(0, TILES) as t:
                    pool.wait_ge(g_idx_ready, t + 1)
                    settled(pool)
                    nc.gpsimd.indirect_dma_start(
                        out=g_x[:, :], out_offset=None, in_=x,
                        in_offset=bass.IndirectOffsetOnAxis(ap=g_idx[:, :], axis=0)).then_inc(g_gathered, 16)
                    pool.wait_ge(g_put_ready, t + 1)
                    settled(pool)
                    nc.gpsimd.indirect_dma_start(
                        out=sums, out_offset=bass.IndirectOffsetOnAxis(ap=g_put[:, :], axis=0),
                        in_=g_v[:, :], in_offset=None, compute_op=ALU.add).then_inc(g_added, 16)

        @block.scalar
        def _(act):
            flat = lambda v: v.rearrange("p c e -> p (c e)")
            act.wait_ge(filled, 1)
            nc.scalar.activation(std[:, 0, 0:1], eps[:, :], ACT.Sqrt).then_inc(table_loaded, 1)
            act.wait_ge(edges_in[2], 64)
            nc.scalar.activation(flat(e_rows[:, 2, :, :]), flat(e_rows_i[:, 2, :, :]), ACT.Copy).then_inc(type_conv, 1)
            act.wait_ge(type_T, 1)
            nc.scalar.activation(type_f[:, :], typeT, ACT.Copy).then_inc(type_sb, 1)
            act.wait_ge(edges_in[0], 48)
            nc.scalar.activation(flat(e_rows[:, 0, 1:CHUNKS, :]), flat(e_rows_i[:, 0, 1:CHUNKS, :]), ACT.Copy).then_inc(srcs_conv, 1)
            act.wait_ge(srcs_T, 1)
            nc.scalar.activation(src_i[:, P:], srcT, ACT.Copy).then_inc(srcs_i, 1)

            def stage(i, q):
                if static(i, 1) and q == 0:
                    act.wait_ge(src0_i, 1)
                    act.wait_ge(srcs_i, 1)
                nc.scalar.activation(idx[:, q * GT:(q + 1) * GT], src_i[:, bass.ds(i * IT + q * GT, GT)],
                                     ACT.Copy).then_inc(idx_ready, 1)

            def deviations(k, q, lo, m):
                act.wait_ge(aggr_done, k + 1)
                nc.scalar.activation(std[:, q, lo:m], mv[:, q, lo:m, 1], ACT.Sqrt, bias=eps[:, :]).then_inc(std_ready, 1)
                act.wait_ge(norm_ready, k + 1)

            def normalise(i, q, n, own):
                g = i * GROUPS + q
                deviations(g if n else GALL, q, 0 if n else GT, GT + own)
                if n and not static(i):
                    act.wait_ge(group_summed, g - GROUPS + 1)
                for j in range(n):
                    t = q * GT + j
                    nc.scalar.activation(hg[:, t, :], xg[:, t, :], ACT.Relu, bias=nmr[:, q, j:j + 1],
                                         scale=rstd[:, q, j:j + 1]).then_inc(h_ready, 1)

            def counts_out(b):
                act.wait_ge(summed, b + 1)
                if not static(b):
                    act.wait_ge(cnt_T, b)
                nc.scalar.activation(cnt_row[:, :], ring[0:1, 1, bass.ds((b % RING) * SEG, SEG)],
                                     ACT.Copy).then_inc(cnt_sb, 1)

            def own(b, q):
                n = rows_of(b)
                if not static(b):
                    act.wait_ge(own_T, b)
                nc.scalar.activation(h_own[0:n, :], x_own[0:n, :], ACT.Relu, bias=nmr[0:n, q, GT:GT + 1],
                                     scale=rstd[0:n, q, GT:GT + 1]).then_inc(own_h, 1)

            def own_copies(b):
                n = rows_of(b)
                act.wait_ge(own_T, b + 1)
                if not static(b):
                    act.wait_ge(z_done, b)
                nc.scalar.activation(hT[:, 0:n], zp[:, 0:n], ACT.Copy).then_inc(own_sb, 1)
                act.wait_ge(inv_T, b + 1)
                if not static(b):
                    act.wait_ge(inv_spread, b)
                nc.scalar.activation(invT[:, :], finT[0:PARTS * R, 0:BLK], ACT.Copy).then_inc(inv_sb, 1)

            def clear_slot(b):
                act.wait_ge(means_ready, b + 1)
                for a in range(2):
                    nc.scalar.activation(ring[:, a, bass.ds((b % RING) * SEG, SEG)], zeros[:, :],
                                         ACT.Copy).then_inc(slot_clear, 1)

            def iteration(i):
                b, done = block_of(i), block_of(i, LAG + 1)
                for q in range(GROUPS):
                    n = tiles_in(i, q)
                    own_here = int(q == OWN_AT and b is not None)
                    if n or own_here:
                        normalise(i, q, n, own_here)
                    if not static(i, ITERS - 1) and tiles_in(i + 1, q):
                        stage(i + 1, q)
                    if q == 1 and done is not None:
                        clear_slot(done)
                    if q == 1 and b is not None:
                        counts_out(b)
                    if q == OWN_AT and b is not None:
                        own(b, q)
                    if q == 4 and b is not None:
                        own_copies(b)

            run_iterations(act, iteration)
            for b in range(BLOCKS - LAG, BLOCKS):
                deviations(GALL + b - BLOCKS + LAG + 1, OWN_AT, GT, GT + 1)
                counts_out(b)
                own(b, OWN_AT)
                own_copies(b)

            act.wait_ge(flag_ready, 1)
            general = act.value_load(flag[0:1, 0:1], min_val=0, max_val=1)
            with act.If(general):
                def h_of(k, src_t, dst_t, n):
                    act.wait_ge(g_var, k + 1)
                    nc.scalar.activation(g_col[0:n, 2:3], g_col[0:n, 1:2], ACT.Sqrt, bias=eps[0:n, :]).then_inc(g_std, 1)
                    act.wait_ge(g_norm, k + 1)
                    nc.scalar.activation(dst_t[0:n, 0:F], src_t[0:n, 0:F], ACT.Relu, bias=g_col[0:n, 4:5],
                                         scale=g_col[0:n, 3:4]).then_inc(g_h_ready, 1)

                with act.Fori(0, TILES) as t:
                    h_of(t, g_x, g_h, P)

                def block_h(b, n):
                    h_of(b + TILES, x_own, h_own, n)
                    act.wait_ge(g_own_T, b + 1)
                    nc.scalar.activation(hT[:, 0:n], zp[:, 0:n], ACT.Copy).then_inc(g_own_sb, 1)
                    act.wait_ge(g_T, b + 1)
                    settled(act)
                    for r in range(R):
                        at = (r % (R // 2)) * BLK
                        nc.scalar.activation(means[:, r, 0:n], fin[:, r // (R // 2), at:at + n], ACT.Copy).then_inc(g_means_sb, 1)

                with act.Fori(0, BLOCKS - 1) as b:
                    block_h(b, BLK)
                block_h(BLOCKS - 1, LASTN)

        @block.vector
        def _(dve):
            nc.vector.memset(eps[:, :], EPS).then_inc(filled, 1)
            nc.vector.memset(zeros[:, :], 0.0).then_inc(filled, 1)
            nc.vector.memset(first[:, :], 0.0).then_inc(first_zero, 1)
            dve.wait_ge(src0_in, 16)
            nc.vector.tensor_copy(e_rows[:, 0, 0, :], e_rows_i[:, 0, 0, :]).then_inc(src0_f, 1)
            nc.vector.memset(ones[:, :], 1.0).then_inc(filled, 1)
            nc.vector.memset(ones_bf[:, :], 1.0).then_inc(filled, 1)
            dve.wait_ge(first_zero, 1)
            nc.vector.memset(first[0:1, :], 1.0).then_inc(filled, 1)
            dve.wait_ge(src0_T, 1)
            nc.vector.tensor_copy(idx[:, :], zp[:, 0:IT]).then_inc(idx_ready, GROUPS)
            nc.vector.tensor_copy(src_i[:, 0:P], zp[:, 0:P]).then_inc(src0_i, 1)
            dve.wait_ge(edges_in[1], 64)
            nc.vector.tensor_copy(e_rows[:, 1, :, :], e_rows_i[:, 1, :, :]).then_inc(dst_conv, 1)
            nc.vector.memset(ring[:, :, :], 0.0).then_inc(filled, 1)
            nc.vector.memset(mv[:, :, :, :], 1.0).then_inc(filled, 1)
            dve.wait_ge(dst_T, 1)
            nc.vector.tensor_copy(dst_f[:, :], dstT).then_inc(dst_sb, 1)
            dve.wait_ge(base_T, 1)
            nc.vector.tensor_scalar(base8[:, :], baseT, float(R), None, ALU.mult).then_inc(base_ready, 1)
            nc.vector.tensor_copy(base_i[:, :], baseT[0:1, :]).then_inc(base_ready, 1)
            dve.wait_ge(type_sb, 1)
            nc.vector.scalar_tensor_tensor(out=seg_f[:, :], in0=dstT, scalar=float(R), in1=type_f[:, :],
                                           op0=ALU.mult, op1=ALU.add).then_inc(seg_ready, 1)
            dve.wait_ge(base_ready, 2)
            dve.wait_ge(seg_ready, 1)
            rels = rel_f[:, :].rearrange("p (g j) -> p g j", j=GT)
            nc.vector.tensor_tensor(rels, seg_f[:, 0:TILES].rearrange("p (g j) -> p g j", j=GT),
                                    base8[:, :].unsqueeze(2).to_broadcast([P, GALL, GT]),
                                    ALU.subtract).then_inc(rel_ready, 1)
            dve.wait_ge(iota_made, 1)
            dve.wait_ge(rel_ready, 1)
            dve.wait_ge(filled, 7)

            def onehots_and_stats(i, q, n, between):
                g = i * GROUPS + q
                if not static(i):
                    dve.wait_ge(group_summed, g - GROUPS + 1)
                for j in range(n):
                    t = q * GT + j
                    a, e = WINDOWS[j]
                    if between:
                        between.pop(0)()
                    nc.vector.tensor_scalar(onehot[:, t, 0:(e - a) * R], iota[:, a * R:e * R],
                                            rel_f[:, bass.ds(i * IT + t, 1)], None,
                                            ALU.is_equal).then_inc(onehot_ready, 1)
                    dve.wait_ge(gathered[t], 16 * (i + 1))
                    nc.vector.bn_stats(stats[:, q, j, :], xg[:, t, :]).then_inc(stats_done, 1)

            def own_stats(b, q):
                n = rows_of(b)
                dve.wait_ge(own_in, 16 * (b + 1))
                nc.vector.bn_stats(stats[0:n, q, GT, :], x_own[0:n, :]).then_inc(stats_done, 1)

            def aggregate(q, n, own, total):
                dve.wait_ge(stats_done, total)
                settled(dve)
                parts = [(j, P) for j in range(n)] + ([(GT, own)] if own else [])
                for j, p in parts:
                    last = nc.vector.bn_aggr(mv[0:p, q, j, :], stats[0:p, q, j, :])
                last.then_inc(aggr_done, 1)

            def scales(k, q, lo, m):
                dve.wait_ge(std_ready, k + 1)
                nc.vector.reciprocal(rstd[:, q, lo:m], std[:, q, lo:m]).then_inc(rstd_done, 1)
                dve.wait_ge(rstd_done, k + 1)
                nc.vector.scalar_tensor_tensor(out=nmr[:, q, lo:m], in0=mv[:, q, lo:m, 0], scalar=-1.0,
                                               in1=rstd[:, q, lo:m], op0=ALU.mult, op1=ALU.mult).then_inc(norm_ready, 1)

            def segment_of(g):
                return (dve.value_load(base_i[0:1, bass.ds(g, 1)], min_val=0, max_val=N - 1) % (RING * BLK)) * R

            def add_group(g, start, q, n, cleared):
                width = WINDOWS[n - 1][1] * R
                at = bass.ds(start, width)
                if cleared is not None:
                    dve.wait_ge(slot_clear, cleared)
                if not static(g):
                    dve.wait_ge(group_added, g)
                dve.wait_ge(group_summed, g + 1)
                nc.vector.tensor_tensor(ring[:, :, at], ring[:, :, at], acc[:, q, :, 0:width],
                                        ALU.add).then_inc(group_added, 1)

            def finish_sums(b, groups):
                dve.wait_ge(group_added, groups)

                def fold():
                    k = b // RING
                    nc.vector.tensor_tensor(ring[:, :, 0:WIN], ring[:, :, 0:WIN], ring[:, :, SPAN:],
                                            ALU.add).then_inc(fold_done, 1)
                    dve.wait_ge(fold_done, 2 * k + 1)
                    nc.vector.memset(ring[:, :, SPAN:], 0.0).then_inc(fold_done, 1)
                    dve.wait_ge(fold_done, 2 * k + 2)
                    settled(dve)

                if not isinstance(b, int):
                    with dve.If((b % RING) == 0):
                        fold()
                elif b % RING == 0:
                    fold()
                dve.sem_inc(summed, 1)

            def inverse_counts(b):
                dve.wait_ge(cnt_T, b + 1)
                if not static(b):
                    dve.wait_ge(inv_T, b)
                nc.vector.tensor_scalar(inv[:, :], fin[0:BLK, 0, 0:R], 1.0, None, ALU.max).then_inc(inv_step, 1)
                dve.wait_ge(inv_step, INV_STEPS * b + 1)
                settled(dve)
                nc.vector.reciprocal(inv[:, :], inv[:, :]).then_inc(inv_step, 1)

            def inverse_parts(b):
                def after(k, ins_of, s):
                    def step():
                        dve.wait_ge(inv_step, INV_STEPS * b + k)
                        ins_of().then_inc(s, 1)
                    return step

                return [
                    after(2, lambda: nc.vector.tensor_copy(inv_parts[:, 0, :], inv[:, :]), inv_step),
                    after(3, lambda: nc.vector.tensor_tensor(rest[:, :], inv[:, :], inv_parts[:, 0, :], ALU.subtract), inv_step),
                    after(4, lambda: nc.vector.tensor_copy(inv_parts[:, 1, :], rest[:, :]), inv_step),
                    after(5, lambda: nc.vector.tensor_tensor(inv_parts[:, 2, :], rest[:, :], inv_parts[:, 1, :], ALU.subtract), inv_ready),
                ]

            def mean_sums(b):
                dve.wait_ge(inv_spread, b + 1)
                if not static(b):
                    dve.wait_ge(z_done, b)
                nc.vector.tensor_tensor(
                    means[:, :, :].rearrange("p (a r) n -> p a r n", a=2),
                    ring[:, 0, bass.ds((b % RING) * SEG, SEG)].rearrange("p (n a r) -> p a r n", r=R // 2, a=2),
                    fin[:, :, 0:SEG // 2].rearrange("p a (r n) -> p a r n", r=R // 2),
                    ALU.mult).then_inc(means_ready, 1)

            def finish_output(b):
                n = rows_of(b)
                dve.wait_ge(z_done, b + 1)
                if not static(b):
                    dve.wait_ge(stored, 16 * b)
                nc.vector.tensor_tensor(y[0:n, :], zp[0:n, 0:F], x_own[0:n, :], ALU.add).then_inc(y_ready, 1)

            def iteration(i):
                b, done = block_of(i), block_of(i, LAG + 1)
                for q in range(GROUPS):
                    n = tiles_in(i, q)
                    g = i * GROUPS + q
                    own = BLK if q == OWN_AT and b is not None else 0
                    adds = not (isinstance(g, int) and (g < 2 or g - 2 >= GALL))
                    start = segment_of(g - 2) if adds else None
                    between = inverse_parts(b) if q == 3 and b is not None else []
                    if n:
                        onehots_and_stats(i, q, n, between)
                    if own:
                        own_stats(b, q)
                    if n or own:
                        owns = 0 if b is None else (b + 1 if q >= OWN_AT else b)
                        tiles = min(TILES, i * IT + q * GT + n) if isinstance(i, int) else i * IT + q * GT + n
                        aggregate(q, n, own, tiles + owns)
                    for step in between:
                        step()
                    if q == 0 and done is not None:
                        mean_sums(done)
                    if q == 1 and done is not None:
                        finish_output(done)
                    if adds:
                        at = (i - 1, q + 3) if q < 2 else (i, q - 2)
                        add_group(g - 2, start, at[1], tiles_in(*at), 2 * (done + 1) if q == 2 and done is not None else None)
                    if q == 1 and b is not None:
                        finish_sums(b, i * GROUPS)
                    if q == 2 and b is not None:
                        inverse_counts(b)
                    if n or own:
                        scales(g if n else GALL, q, 0 if n else GT, GT + (1 if own else 0))

            def check_order():
                cols = []

                def extreme(values, p, op, limit, neutral=None):
                    c = len(cols)
                    if neutral is not None:
                        nc.vector.memset(ext[:, c:c + 1], neutral).then_inc(check_step, 1)
                        steps[0] += 1
                        dve.wait_ge(check_step, steps[0])
                    nc.vector.tensor_reduce(ext[0:p, c:c + 1], values, AX.X, op).then_inc(check_step, 1)
                    steps[0] += 1
                    cols.append((limit, ALU.is_gt if op == ALU.max else ALU.is_lt))

                steps = [0]
                dve.wait_ge(low_made, 1)
                nc.vector.tensor_tensor(dev8[:, :], base8[:, :], lin8[:, 0:GALL], ALU.subtract).then_inc(check_step, 1)
                steps[0] += 1
                for j, (a, e) in enumerate(WINDOWS):
                    groups = GALL - (j == GT - 1)
                    for op, limit in ((ALU.max, e * R - 0.5), (ALU.min, a * R - 0.5)):
                        extreme(rels[:, 0:groups, j], P, op, limit)
                a, e = WINDOWS[GT - 1]
                for op, limit in ((ALU.max, e * R - 0.5), (ALU.min, a * R - 0.5)):
                    extreme(rel_f[0:EDGES_L, TILES - 1:TILES], EDGES_L, op, limit, float(a * R))
                dve.wait_ge(check_step, steps[0])
                for op, limit in ((ALU.max, LIVE * SEG - WIN + 0.5), (ALU.min, -0.5)):
                    extreme(dev8[:, :], P, op, limit)
                dve.wait_ge(check_step, steps[0])
                for c, (limit, cmp) in enumerate(cols):
                    last = nc.vector.tensor_scalar(bad[:, c:c + 1], ext[:, c:c + 1], limit, None, cmp)
                last.then_inc(check_step, 1)
                steps[0] += 1
                dve.wait_ge(check_step, steps[0])
                assert len(cols) == CHECKS
                nc.vector.tensor_reduce(bad1[:, :], bad[:, :], AX.X, ALU.max).then_inc(bad_ready, 1)
                dve.wait_ge(bad_sum, 1)
                nc.vector.tensor_scalar(flag[:, :], zp[0:1, 0:1], 1.0, None, ALU.min).then_inc(flag_ready, 1)

            iteration(0)
            check_order()
            for i in range(1, LAG + 2):
                iteration(i)
            with dve.Fori(LAG + 2, ITERS - 1) as i:
                iteration(i)
            iteration(ITERS - 1)
            mean_sums(BLOCKS - LAG - 1)
            finish_output(BLOCKS - LAG - 1)
            for b in range(BLOCKS - LAG, BLOCKS):
                k = GALL + b - BLOCKS + LAG + 1
                own_stats(b, OWN_AT)
                aggregate(OWN_AT, 0, rows_of(b), TILES + b + 1)
                finish_sums(b, GALL)
                scales(k, OWN_AT, GT, GT + 1)
                inverse_counts(b)
                for step in inverse_parts(b):
                    step()
                mean_sums(b)
                finish_output(b)

            dve.wait_ge(flag_ready, 1)
            general = dve.value_load(flag[0:1, 0:1], min_val=0, max_val=1)
            with dve.If(general):
                def chained(ins, k):
                    ins.then_inc(g_step, 1)
                    dve.wait_ge(g_step, k)
                    settled(dve)

                chained(nc.vector.memset(g_h[:, F:VW], 0.0), 1)
                chained(nc.vector.memset(g_h[:, F:F + 1], 1.0), 2)
                dve.wait_ge(g_const, 3)

                def mean_var(k, step, src_t, n):
                    chained(nc.vector.bn_stats(stats[0:n, 0, 0, :], src_t[0:n, 0:F]), step + 1)
                    nc.vector.bn_aggr(g_col[0:n, 0:2], stats[0:n, 0, 0, :]).then_inc(g_var, 1)
                    dve.wait_ge(g_std, k + 1)
                    settled(dve)
                    chained(nc.vector.reciprocal(g_col[0:n, 3:4], g_col[0:n, 2:3]), step + 2)
                    nc.vector.scalar_tensor_tensor(out=g_col[0:n, 4:5], in0=g_col[0:n, 0:1], scalar=-1.0,
                                                   in1=g_col[0:n, 3:4], op0=ALU.mult, op1=ALU.mult).then_inc(g_norm, 1)

                TILE_STEPS = 7
                with dve.Fori(0, TILES) as t:
                    s0 = 2 + t * TILE_STEPS
                    dve.wait_ge(g_added, 16 * (t + 1))
                    settled(dve)
                    nc.vector.tensor_copy(g_idx[:, :], src_i[:, bass.ds(t, 1)]).then_inc(g_idx_ready, 1)
                    key = seg_f[:, bass.ds(t, 1)]
                    nc.vector.tensor_scalar(g_key[:, :], ones[:, :], key, None, ALU.mult).then_inc(g_keys, 1)
                    dve.wait_ge(g_spread, t + 1)
                    nc.vector.tensor_scalar(g_eq[:, :], fin[:, 0, 0:P], key, None, ALU.is_equal).then_inc(g_eq_ready, 1)
                    dve.wait_ge(g_eq_ready, t + 1)
                    chained(nc.vector.tensor_tensor(g_tmp[:, :], g_eq[:, :], g_low[:, :], ALU.mult), s0 + 1)
                    chained(nc.vector.tensor_reduce(g_col[:, 5:6], g_tmp[:, :], AX.X, ALU.add), s0 + 2)
                    chained(nc.vector.tensor_scalar(g_col[:, 5:6], g_col[:, 5:6], 0.5, None, ALU.is_lt), s0 + 3)
                    chained(nc.vector.scalar_tensor_tensor(out=g_col[:, 6:7], in0=key, scalar=-0.5, in1=g_col[:, 5:6],
                                                           op0=ALU.is_gt, op1=ALU.mult), s0 + 4)
                    chained(nc.vector.tensor_tensor(g_col[:, 7:8], key, g_row[:, :], ALU.subtract), s0 + 5)
                    nc.vector.scalar_tensor_tensor(out=g_put[:, :], in0=g_col[:, 6:7], scalar=g_col[:, 7:8],
                                                   in1=g_row[:, :], op0=ALU.mult, op1=ALU.add).then_inc(g_put_written, 1)
                    dve.wait_ge(g_gathered, 16 * (t + 1))
                    settled(dve)
                    mean_var(t, s0 + 5, g_x, P)
                    dve.wait_ge(g_put_written, t + 1)
                    dve.wait_ge(g_summed, t + 1)
                    settled(dve)
                    nc.vector.tensor_copy(g_v[:, :], fin[:, 1, 0:VW]).then_inc(g_put_ready, 1)

                def block_means(b, n, first_step):
                    dve.wait_ge(g_in, 16 * (b + 1))
                    settled(dve)
                    mean_var(b + TILES, first_step, x_own, n)
                    dve.wait_ge(g_sums_in, 16 * (b + 1))
                    settled(dve)
                    chained(nc.vector.tensor_scalar(g_c[0:n, :], g_s[0:n, :, F], 1.0, None, ALU.max), first_step + 3)
                    chained(nc.vector.reciprocal(g_c[0:n, :], g_c[0:n, :]), first_step + 4)
                    for r in range(R):
                        last = nc.vector.tensor_scalar(g_s[0:n, r, 0:F], g_s[0:n, r, 0:F], g_c[0:n, r:r + 1], None, ALU.mult)
                    last.then_inc(g_means, 1)
                    dve.wait_ge(g_z, b + 1)
                    settled(dve)
                    nc.vector.tensor_tensor(y[0:n, :], zp[0:n, 0:F], x_own[0:n, :], ALU.add).then_inc(g_y, 1)

                done = 2 + TILES * TILE_STEPS
                with dve.Fori(0, BLOCKS - 1) as b:
                    block_means(b, BLK, done + 4 * b)
                block_means(BLOCKS - 1, LASTN, done + 4 * (BLOCKS - 1))

        @block.tensor
        def _(pe):
            pe.wait_ge(ident_made, 2)
            pe.wait_ge(src0_f, 1)
            nc.tensor.transpose(zp[:, 0:P], e_rows[:, 0, 0, :], ident[:, :]).then_inc(src0_T, 1)

            def transposes(to, a, c0, done):
                for c in range(c0, CHUNKS):
                    last = nc.tensor.transpose(to[:, (c - c0) * P:(c - c0 + 1) * P], e_rows[:, a, c, :], ident[:, :])
                last.then_inc(done, 1)

            pe.wait_ge(dst_conv, 1)
            transposes(dstT, 1, 0, dst_T)
            pe.wait_ge(dst_sb, 1)
            pe.wait_ge(filled, 5)
            nc.tensor.matmul(baseT, first[:, :], dst_f[:, 0:TILES].rearrange("p (g j) -> p g j", j=GT)[:, :, 0],
                             start=True, stop=True).then_inc(base_T, 1)
            pe.wait_ge(type_conv, 1)
            transposes(typeT, 2, 0, type_T)
            pe.wait_ge(srcs_conv, 1)
            transposes(srcT, 0, 1, srcs_T)
            pe.wait_ge(seg_ready, 1)
            pe.wait_ge(base_ready, 2)

            def sums_of(i, q, n):
                g = i * GROUPS + q
                if not static(i):
                    pe.wait_ge(group_added, g - GROUPS + 1)
                for j in range(n):
                    t = q * GT + j
                    a, e = WINDOWS[j]
                    at, width = slice(a * R, e * R), (e - a) * R
                    pe.wait_ge(h_ready, i * IT + t + 1)
                    pe.wait_ge(onehot_ready, i * IT + t + 1)
                    nc.tensor.matmul(acc[:, q, 0, at], hg[:, t, :], onehot[:, t, 0:width],
                                     start=(j == 0), stop=(j == n - 1), skip_group_check=True)
                    halves = onehot[:, t, 0:width].bitcast(bf16).rearrange("p (w h) -> p w h", h=2)[:, :, 1]
                    last = nc.tensor.matmul(acc[:, q, 1, at], ones_bf[:, :], halves,
                                            start=False, stop=(j == n - 1), skip_group_check=True)
                last.then_inc(group_summed, 1)

            def counts_to_nodes(b):
                pe.wait_ge(cnt_sb, b + 1)
                if not static(b):
                    pe.wait_ge(means_ready, b)
                settled(pe)
                cnt = cnt_row[:, :].rearrange("p (n r) -> p n r", r=R)
                for r in range(R):
                    last = nc.tensor.transpose(fin[0:BLK, 0, r:r + 1], cnt[:, :, r], ident[0:1, 0:1])
                last.then_inc(cnt_T, 1)

            def own_transposes(b):
                n = rows_of(b)
                pe.wait_ge(own_h, b + 1)
                if not static(b):
                    pe.wait_ge(y_ready, b)
                nc.tensor.transpose(zp[:, 0:n], h_own[0:n, :], ident[0:n, 0:n]).then_inc(own_T, 1)
                pe.wait_ge(inv_ready, b + 1)
                nc.tensor.transpose(finT[0:PARTS * R, 0:BLK], inv_parts[:, :, :].rearrange("n k r -> n (k r)"),
                                    ident_bf[0:BLK, 0:BLK]).then_inc(inv_T, 1)

            def spread_inverse(b):
                pe.wait_ge(inv_sb, b + 1)
                for r in range(R):
                    at = (r % (R // 2)) * BLK
                    last = nc.tensor.matmul(fin[:, r // (R // 2), at:at + BLK], pick[:, r, :], invT[:, :],
                                            start=True, stop=True)
                last.then_inc(inv_spread, 1)

            def weights(n):
                for r in range(R):
                    nc.tensor.matmul(zp[0:n, 0:F], means[:, r, 0:n], w_sb[:, r, :], start=(r == 0), stop=False)
                nc.tensor.matmul(zp[0:n, 0:F], hT[:, 0:n], wr_sb[:, :], start=False, stop=False)
                return nc.tensor.matmul(zp[0:n, 0:F], ones[0:1, 0:n], bias_sb[:, :], start=False, stop=True)

            def outputs(b):
                pe.wait_ge(own_sb, b + 1)
                pe.wait_ge(means_ready, b + 1)
                weights(rows_of(b)).then_inc(z_done, 1)

            def iteration(i):
                b = block_of(i)
                for q in range(GROUPS):
                    n = tiles_in(i, q)
                    if n:
                        sums_of(i, q, n)
                    if q == 0 and block_of(i, LAG + 1) is not None:
                        outputs(i - LAG - 1)
                    if b is not None:
                        if q == 1:
                            counts_to_nodes(b)
                        if q == 3:
                            own_transposes(b)
                        if q == 4:
                            spread_inverse(b)

            iteration(0)
            pe.wait_ge(bad_ready, 1)
            nc.tensor.matmul(zp[0:1, 0:1], bad1[:, :], ones[:, 0:1], start=True, stop=True).then_inc(bad_sum, 1)
            pe.wait_ge(srcs_i, 1)
            pe.wait_ge(flag_ready, 1)
            pe.wait_ge(consts_in, 48)
            pe.wait_ge(pick_made, 1 + PARTS)
            pe.wait_ge(ident_made, 3)
            for i in range(1, LAG + 2):
                iteration(i)
            with pe.Fori(LAG + 2, ITERS - 1) as i:
                iteration(i)
            iteration(ITERS - 1)
            outputs(BLOCKS - LAG - 1)
            for b in range(BLOCKS - LAG, BLOCKS):
                counts_to_nodes(b)
                own_transposes(b)
                spread_inverse(b)
                outputs(b)

            general = pe.value_load(flag[0:1, 0:1], min_val=0, max_val=1)
            with pe.If(general):
                with pe.Fori(0, TILES) as t:
                    pe.wait_ge(g_keys, t + 1)
                    nc.tensor.matmul(fin[:, 0, 0:P], g_key[:, :], ident[:, :], start=True, stop=True).then_inc(g_spread, 1)
                    pe.wait_ge(g_eq_ready, t + 1)
                    pe.wait_ge(g_h_ready, t + 1)
                    nc.tensor.matmul(fin[:, 1, 0:VW], g_eq[:, :], g_h[:, :], start=True, stop=True).then_inc(g_summed, 1)

                def block_out(b, n):
                    pe.wait_ge(g_h_ready, b + TILES + 1)
                    nc.tensor.transpose(zp[:, 0:n], h_own[0:n, :], ident[0:n, 0:n]).then_inc(g_own_T, 1)
                    pe.wait_ge(g_means, b + 1)
                    for r in range(R):
                        at = (r % (R // 2)) * BLK
                        last = nc.tensor.transpose(fin[:, r // (R // 2), at:at + n], g_s[0:n, r, 0:F], ident[0:n, 0:n])
                    last.then_inc(g_T, 1)
                    pe.wait_ge(g_own_sb, b + 1)
                    pe.wait_ge(g_means_sb, R * (b + 1))
                    weights(n).then_inc(g_z, 1)

                with pe.Fori(0, BLOCKS - 1) as b:
                    block_out(b, BLK)
                block_out(BLOCKS - 1, LASTN)


_INS = ["x", "src", "dst", "edge_type_8", "L0_gnn_W", "L0_gnn_W_root", "L0_gnn_bias"]


def kernel(**inputs):
    import concourse.bacc as bacc
    from concourse.bass_utils import run_bass_kernel_spmd as run

    nc = bacc.Bacc("TRN2", target_bir_lowering=False, num_devices=1)
    arrays, args = {}, []
    for name in _INS:
        a = np.ascontiguousarray(inputs[name])
        arrays[f"in_{name}"] = a
        args.append(nc.dram_tensor(f"in_{name}", a.shape, mybir.dt.from_np(a.dtype), kind="ExternalInput").ap())
    out = nc.dram_tensor("out_0", (N, F), mybir.dt.float32, kind="ExternalOutput").ap()
    rgcn(nc, *args, out)
    r = run(nc, [arrays], core_ids=[0])
    return r.results[0]["out_0"]
```

```python
from contextlib import ExitStack
from math import ceil, floor, sqrt

import numpy as np

import concourse.bass as bass
from concourse import mybir

P = 128
F = 128
R = 8
N = 6250
E = 106250
TILES = ceil(E / P)
GT = 3
GROUPS = 5
IT = GT * GROUPS
BLK = 112
ITERS = ceil(TILES / IT)
BLOCKS = ceil(N / BLK)
LAG = 2
GALL = ceil(TILES / GT)
ENDG = (ITERS - 1) * GROUPS
LASTB = range(BLOCKS - LAG - 1, BLOCKS)
ENDB = LASTB[0] - 1
LASTN = N - (BLOCKS - 1) * BLK
LP, LC = 125, 50
NORM_CUTS = [0, 4] + list(range(10, 47, 6)) + [50]
NORM_STEPS = len(NORM_CUTS) - 1
LOADS = 8
CH = BLOCKS // LOADS
RING = 5
LIVE = 4
SEG = BLK * R
CHUNKS = ceil(TILES / P)
ROWS_L = TILES - (CHUNKS - 1) * P
EDGES_L = E - (TILES - 1) * P
PAD_DST = -1
EPS = 1e-5
NODES_PER_TILE = N * P / E
FLAT = 6.0


def window(j):
    a, b = j * NODES_PER_TILE, (j + 1) * NODES_PER_TILE
    spread = lambda nodes: FLAT * sqrt(nodes * N / E)
    return max(0, floor(a - spread(a))), ceil(b + 1 + spread(b))


WINDOWS = [window(j) for j in range(GT)]
WIN = WINDOWS[-1][1] * R
OHW = max(b - a for a, b in WINDOWS) * R
SPAN = RING * SEG
TRASH = BLOCKS * SEG
CHECKS = 2 * GT + 5
INV_STEPS = 2
ADDS = R + 1
VW = F + 4
assert 2 * WIN <= 512 and BLOCKS == ITERS and GALL * GT == TILES and GALL == ENDG + 2 and CH * LOADS == BLOCKS
assert LP * LC == N and NORM_CUTS[-1] == LC


def rgcn(nc, x, src, dst, etype, w, w_root, bias, out):
    f32, bf16, i32 = mybir.dt.float32, mybir.dt.bfloat16, mybir.dt.int32
    ALU, ACT, AX = mybir.AluOpType, mybir.ActivationFunctionType, mybir.AxisListType
    table = nc.dram_tensor("h_table", [N, F], f32, kind="Internal").ap()
    sums = nc.dram_tensor("segment_sums", [TRASH + P, VW], f32, kind="Internal").ap()

    with ExitStack() as ctx:
        def sb(name, shape, dt=f32):
            return ctx.enter_context(nc.sbuf_tensor(name, shape, dt))

        def pb(name, shape, dt=f32):
            return ctx.enter_context(nc.psum_tensor(name, shape, dt))

        def sem(name):
            return ctx.enter_context(nc.semaphore(name))

        x_all = sb("x_all", [P, BLOCKS, F])
        h_all = sb("h_all", [P, BLOCKS, F])
        stats = sb("stats", [LP, LC, 6])
        mv = sb("mv", [LP, LC, 2])
        std = sb("std", [LP, LC])
        rstd = sb("rstd", [LP, LC])
        nmr = sb("nmr", [LP, LC])
        t_stats = sb("t_stats", [P, IT, 6])
        t_mv = sb("t_mv", [P, IT, 2])
        t_std = sb("t_std", [P, IT])
        t_rstd = sb("t_rstd", [P, IT])
        t_nmr = sb("t_nmr", [P, IT])
        e_rows_i = sb("e_rows_i", [P, 3, CHUNKS, P], i32)
        e_rows = sb("e_rows", [P, 3, CHUNKS, P])
        src_i = sb("src_i", [P, CHUNKS * P], i32)
        dst_f = sb("dst_f", [P, CHUNKS * P])
        seg_f = sb("seg_f", [P, CHUNKS * P])
        rel_f = sb("rel_f", [P, TILES])
        base8 = sb("base8", [P, GALL])
        near8 = sb("near8", [P, GALL])
        laps = sb("laps", [P, GALL])
        at_i = sb("at_i", [1, GALL], i32)
        idx = sb("idx", [P, IT], i32)
        hg = sb("hg", [P, IT, F])
        onehot = sb("onehot", [P, IT, OHW])
        ring = sb("ring", [P, 2, SPAN + WIN])
        blk = sb("blk", [P, R, BLK])
        cnt_row = sb("cnt_row", [1, SEG])
        cnt = sb("cnt", [BLK, R])
        cnt1 = sb("cnt1", [BLK, R])
        inv = sb("inv", [BLK, R])
        h_own = sb("h_own", [P, F])
        hT = sb("hT", [P, BLK])
        even = sb("even", [BLK, F])
        w_sb = sb("w_sb", [P, R, F])
        wr_sb = sb("wr_sb", [P, F])
        bias_sb = sb("bias_sb", [1, F])
        ident = sb("ident", [P, P])
        first = sb("first", [P, P])
        ones = sb("ones", [P, P])
        ones_bf = sb("ones_bf", [P, P], bf16)
        iota = sb("iota", [P, WIN])
        zeros = sb("zeros", [P, SEG])
        eps = sb("eps", [P, 1])
        laps_at = sb("laps_at", [P, 1])
        low8 = sb("low8", [P, ITERS * GROUPS])
        dev8 = sb("dev8", [P, GALL])
        ext = sb("ext", [P, CHECKS])
        bad = sb("bad", [P, CHECKS])
        bad1 = sb("bad1", [P, 1])
        flag = sb("flag", [1, 1], i32)
        g_idx = sb("g_idx", [P, 1], i32)
        g_put = sb("g_put", [P, 1], i32)
        g_x = sb("g_x", [P, F])
        g_out = sb("g_out", [P, F])
        g_h = sb("g_h", [P, VW])
        g_v = sb("g_v", [P, VW])
        g_key = sb("g_key", [P, P])
        g_eq = sb("g_eq", [P, P])
        g_low = sb("g_low", [P, P])
        g_before = sb("g_before", [P, P])
        g_col = sb("g_col", [P, 3])
        g_row = sb("g_row", [P, 1])
        g_s = sb("g_s", [P, R, VW])
        g_c = sb("g_c", [P, R])

        acc = pb("acc", [P, GROUPS, 2, 256])
        fin = pb("fin", [P, 2, 512])
        zp = pb("zp", [P, 512])
        cntT = zp[0:BLK, P:P + R]

        src0_in, consts_in = sem("src0_in"), sem("consts_in")
        edges_in = [sem("src_in"), sem("dst_in"), sem("type_in")]
        x_in = [sem(f"x_in{c}") for c in range(NORM_STEPS)]
        pads, ident_made, iota_made, laps_made, low_made = (
            sem("pads"), sem("ident_made"), sem("iota_made"), sem("laps_made"), sem("low_made"))
        eps_made, ones_made, first_zero, first_made, zeros_made, ring_cleared = (
            sem("eps_made"), sem("ones_made"), sem("first_zero"), sem("first_made"), sem("zeros_made"), sem("ring_cleared"))
        table_loaded = sem("table_loaded")
        stats_done, aggr_done, std_ready, rstd_done, norm_ready = (
            sem("stats_done"), sem("aggr_done"), sem("std_ready"), sem("rstd_done"), sem("norm_ready"))
        h_ready, h_stored = sem("h_ready"), sem("h_stored")
        t_stats_done, t_aggr_done, t_std_ready, t_rstd_done, t_norm_ready, t_h_ready = (
            sem("t_stats_done"), sem("t_aggr_done"), sem("t_std_ready"), sem("t_rstd_done"), sem("t_norm_ready"), sem("t_h_ready"))
        h_blocks_in, x_blocks_in = sem("h_blocks_in"), sem("x_blocks_in")
        src0_f, dst_conv, type_conv, srcs_conv = sem("src0_f"), sem("dst_conv"), sem("type_conv"), sem("srcs_conv")
        src0_T, dst_T, type_T, srcs_T, base_T, laps_T = (
            sem("src0_T"), sem("dst_T"), sem("type_T"), sem("srcs_T"), sem("base_T"), sem("laps_T"))
        src0_i, srcs_i, dst_sb = sem("src0_i"), sem("srcs_i"), sem("dst_sb")
        seg_ready, base_ready, laps_ready, at_ready, rel_ready = (
            sem("seg_ready"), sem("base_ready"), sem("laps_ready"), sem("at_ready"), sem("rel_ready"))
        near_step = sem("near_step")
        idx_ready, onehot_ready = sem("idx_ready"), sem("onehot_ready")
        gathered = [sem(f"gathered{j}") for j in range(IT)]
        group_summed, group_added = sem("group_summed"), sem("group_added")
        passed = sem("passed")
        fold_done, summed, taken, slot_clear = sem("fold_done"), sem("summed"), sem("taken"), sem("slot_clear")
        own_h, block_T, block_sb, inv_step = sem("own_h"), sem("block_T"), sem("block_sb"), sem("inv_step")
        z_low, z_root, z_high = sem("z_low"), sem("z_root"), sem("z_high")
        term_added, y_ready, stored = sem("term_added"), sem("y_ready"), sem("stored")
        check_step, bad_ready, bad_sum, flag_ready = sem("check_step"), sem("bad_ready"), sem("bad_sum"), sem("flag_ready")
        g_zeroed, g_added, g_step, g_const = sem("g_zeroed"), sem("g_added"), sem("g_step"), sem("g_const")
        g_idx_ready, g_gathered, g_keys, g_spread = sem("g_idx_ready"), sem("g_gathered"), sem("g_keys"), sem("g_spread")
        g_eq_ready, g_summed, g_put_ready, g_put_written = (
            sem("g_eq_ready"), sem("g_summed"), sem("g_put_ready"), sem("g_put_written"))
        g_in, g_sums_in, g_means, g_T = sem("g_in"), sem("g_sums_in"), sem("g_means"), sem("g_T")
        g_own, g_own_T, g_own_sb, g_means_sb, g_z, g_y, g_stored = (
            sem("g_own"), sem("g_own_T"), sem("g_own_sb"), sem("g_means_sb"), sem("g_z"), sem("g_y"), sem("g_stored"))

        block = ctx.enter_context(nc.Block())

        def static(i, value=0):
            return isinstance(i, int) and i == value

        def tiles_in(i, q):
            return GT if not isinstance(i, int) else max(0, min(GT, TILES - i * IT - q * GT))

        def block_of(i, lag):
            return i - lag if not isinstance(i, int) or 0 <= i - lag < BLOCKS else None

        def rows_of(b):
            return LASTN if static(b, BLOCKS - 1) else BLK

        def terms_before(b):
            return (ADDS - 1) * b + (max(0, b - ENDB) if isinstance(b, int) else 0)

        def settled(eng):
            eng.sem_inc(passed, 1)

        def run_iterations(eng, iteration, end, after_first=lambda: None):
            iteration(0)
            after_first()
            for i in range(1, LAG + 2):
                iteration(i)
            with eng.Fori(LAG + 2, ITERS - 1) as i:
                iteration(i)
            end()

        acc_flat = acc[:, :, :, :].rearrange("p q a w -> p (q a w)")
        dstT = acc_flat[:, 0:CHUNKS * P]
        typeT = acc_flat[:, 1024:1024 + CHUNKS * P]
        baseT = acc_flat[:, 2048:2048 + GALL]
        fin_flat = fin[:, :, :].rearrange("p a w -> p (a w)")
        srcT = fin_flat[:, 0:(CHUNKS - 1) * P]
        lapsT = zp[0:1, 0:GALL]

        @block.sync
        def _(sp):
            def chunk0(a, v, s):
                sp.dma_start(e_rows_i[:, a, 0, :], v[0:P * P].rearrange("(t e) -> t e", e=P)).then_inc(s, 16)

            def chunks(a, v):
                if a:
                    chunk0(a, v, edges_in[a])
                sp.dma_start(e_rows_i[:, a, 1:CHUNKS - 1, :], v[P * P:(CHUNKS - 1) * P * P]
                             .rearrange("(c t e) -> t c e", t=P, e=P)).then_inc(edges_in[a], 16)
                sp.dma_start(e_rows_i[0:ROWS_L - 1, a, CHUNKS - 1, :],
                             v[(CHUNKS - 1) * P * P:(TILES - 1) * P].rearrange("(t e) -> t e", e=P)).then_inc(edges_in[a], 16)
                sp.dma_start(e_rows_i[ROWS_L - 1:ROWS_L, a, CHUNKS - 1, 0:EDGES_L],
                             v[(TILES - 1) * P:E].rearrange("(t e) -> t e", t=1)).then_inc(edges_in[a], 16)

            x_rows = x.rearrange("(p c) f -> p c f", c=LC)
            table_rows = table.rearrange("(p c) f -> p c f", c=LC)

            def load_x(k):
                at = slice(NORM_CUTS[k], NORM_CUTS[k + 1])
                sp.dma_start(x_all[0:LP, at, :], x_rows[:, at, :]).then_inc(x_in[k], 16)

            chunk0(0, src, src0_in)
            load_x(0)
            load_x(1)
            sp.wait_ge(pads, 3)
            chunks(1, dst)
            load_x(2)
            load_x(3)
            chunks(2, etype)
            for k in range(4, NORM_STEPS):
                load_x(k)
            chunks(0, src)
            for k in range(NORM_STEPS):
                at = slice(NORM_CUTS[k], NORM_CUTS[k + 1])
                sp.wait_ge(h_ready, NORM_CUTS[k + 1])
                sp.dma_start(table_rows[:, at, :], h_all[0:LP, at, :]).then_inc(h_stored, 16)
            sp.dma_start(w_sb[:, :, :], w.rearrange("r k n -> k r n")).then_inc(consts_in, 16)
            sp.dma_start(wr_sb[:, :], w_root).then_inc(consts_in, 16)
            sp.dma_start(bias_sb[:, :], bias.rearrange("(a n) -> a n", a=1)).then_inc(consts_in, 16)
            sp.wait_ge(h_stored, 16 * NORM_STEPS)
            for step, (dest, rows, done) in enumerate(((h_all, table, h_blocks_in), (x_all, x, x_blocks_in))):
                for c in range(LOADS):
                    full = CH - (c == LOADS - 1)
                    sp.wait_ge(group_summed, step * LOADS + c + 1)
                    sp.dma_start(dest[0:BLK, c * CH:c * CH + full, :], rows[c * CH * BLK:(c * CH + full) * BLK, :]
                                 .rearrange("(b n) f -> n b f", n=BLK)).then_inc(done, 16)
                sp.wait_ge(pads, 5)
                sp.dma_start(dest[0:LASTN, BLOCKS - 1, :], rows[(BLOCKS - 1) * BLK:N, :]).then_inc(done, 16)

            def store(b, n):
                sp.wait_ge(y_ready, b + 1)
                sp.dma_start(out[bass.ds(b * BLK, n), :],
                             x_all[0:n, bass.ds(b, 1), :].rearrange("p a f -> p (a f)")).then_inc(stored, 16)

            with sp.Fori(0, BLOCKS - 1) as b:
                store(b, BLK)
            store(BLOCKS - 1, LASTN)
            sp.wait_ge(stored, 16 * BLOCKS)

            sp.wait_ge(flag_ready, 1)
            general = sp.value_load(flag[0:1, 0:1], min_val=0, max_val=1)
            with sp.If(general):
                sp.dma_start(sums.rearrange("(p a) c -> p a c", p=P),
                             zeros[:, 0:VW].unsqueeze(1).to_broadcast([P, (TRASH + P) // P, VW])).then_inc(g_zeroed, 16)
                sp.wait_ge(g_added, 16 * TILES)

                def block_io(b, n, before):
                    if before is not None:
                        sp.wait_ge(g_stored, before)
                    sp.dma_start(g_s[0:n, :, :], sums[bass.ds(b * SEG, n * R), :]
                                 .rearrange("(n r) c -> n r c", r=R)).then_inc(g_sums_in, 16)
                    sp.dma_start(g_x[0:n, :], x[bass.ds(b * BLK, n), :]).then_inc(g_in, 16)
                    sp.wait_ge(g_y, b + 1)
                    sp.dma_start(out[bass.ds(b * BLK, n), :], g_out[0:n, :]).then_inc(g_stored, 16)

                block_io(0, BLK, None)
                with sp.Fori(1, BLOCKS - 1) as b:
                    block_io(b, BLK, 16 * b)
                block_io(BLOCKS - 1, LASTN, 16 * (BLOCKS - 1))
                sp.wait_ge(g_stored, 16 * BLOCKS)
                settled(sp)

        @block.gpsimd
        def _(pool):
            nc.gpsimd.memset(ident[:, :], 0.0).then_inc(ident_made, 1)
            pool.wait_ge(ident_made, 1)
            nc.gpsimd.affine_select(out=ident[:, :], in_=ident[:, :], compare_op=ALU.not_equal, fill=1.0,
                                    base=0, pattern=[[-1, P]], channel_multiplier=1).then_inc(ident_made, 1)
            for a, v in ((0, 0), (1, PAD_DST), (2, 0)):
                nc.gpsimd.memset(e_rows_i[:, a, CHUNKS - 1, :], v).then_inc(pads, 1)
            for nodes in (x_all, h_all):
                nc.gpsimd.memset(nodes[:, BLOCKS - 1, :], 0.0).then_inc(pads, 1)
            nc.gpsimd.iota(iota[:, :], [[1, WIN]], base=0, channel_multiplier=0,
                           allow_small_or_imprecise_dtypes=True).then_inc(iota_made, 1)
            nc.gpsimd.iota(laps_at[:, :], [[1, 1]], base=SPAN, channel_multiplier=SPAN,
                           allow_small_or_imprecise_dtypes=True).then_inc(laps_made, 1)
            nc.gpsimd.iota(low8[:, :], [[SEG, ITERS], [0, GROUPS]], base=-SEG, channel_multiplier=0,
                           allow_small_or_imprecise_dtypes=True).then_inc(low_made, 1)
            nc.gpsimd.memset(first[:, :], 0.0).then_inc(first_zero, 1)
            nc.gpsimd.memset(zeros[:, :], 0.0).then_inc(zeros_made, 1)
            nc.gpsimd.memset(ones[:, :], 1.0).then_inc(ones_made, 1)
            nc.gpsimd.memset(ones_bf[:, :], 1.0).then_inc(ones_made, 1)
            pool.wait_ge(first_zero, 1)
            nc.gpsimd.memset(first[0:1, :], 1.0).then_inc(first_made, 1)
            def gathers(i, n):
                for j in range(n):
                    if j % GT == 0:
                        pool.wait_ge(idx_ready, i * GROUPS + j // GT + 1)
                        settled(pool)
                    nc.gpsimd.indirect_dma_start(
                        out=hg[:, j, :], out_offset=None, in_=x if static(i) else table,
                        in_offset=bass.IndirectOffsetOnAxis(ap=idx[:, j:j + 1], axis=0)).then_inc(gathered[j], 16)
                    if static(i) and j == GT - 1:
                        pool.wait_ge(edges_in[1], 64)
                        nc.gpsimd.tensor_copy(e_rows[:, 1, :, :], e_rows_i[:, 1, :, :]).then_inc(dst_conv, 1)

            gathers(0, IT)
            nc.gpsimd.memset(ring[:, :, :], 0.0).then_inc(ring_cleared, 1)
            pool.wait_ge(h_stored, 16 * NORM_STEPS)
            with pool.Fori(1, ITERS - 1) as i:
                gathers(i, IT)
            gathers(ITERS - 1, TILES - (ITERS - 1) * IT)

            pool.wait_ge(flag_ready, 1)
            general = pool.value_load(flag[0:1, 0:1], min_val=0, max_val=1)
            with pool.If(general):
                nc.gpsimd.memset(g_low[:, :], 1.0).then_inc(g_const, 1)
                pool.wait_ge(g_const, 1)
                nc.gpsimd.affine_select(out=g_low[:, :], in_=g_low[:, :], compare_op=ALU.is_gt, fill=0.0,
                                        base=0, pattern=[[-1, P]], channel_multiplier=1).then_inc(g_const, 1)
                nc.gpsimd.iota(g_row[:, :], [[1, 1]], base=TRASH, channel_multiplier=1,
                               allow_small_or_imprecise_dtypes=True).then_inc(g_const, 1)
                pool.wait_ge(g_zeroed, 16)
                with pool.Fori(0, TILES) as t:
                    pool.wait_ge(g_idx_ready, t + 1)
                    settled(pool)
                    nc.gpsimd.indirect_dma_start(
                        out=g_h[:, 0:F], out_offset=None, in_=table,
                        in_offset=bass.IndirectOffsetOnAxis(ap=g_idx[:, :], axis=0)).then_inc(g_gathered, 16)
                    pool.wait_ge(g_put_ready, t + 1)
                    settled(pool)
                    nc.gpsimd.indirect_dma_start(
                        out=sums, out_offset=bass.IndirectOffsetOnAxis(ap=g_put[:, :], axis=0),
                        in_=g_v[:, :], in_offset=None, compute_op=ALU.add).then_inc(g_added, 16)

        @block.scalar
        def _(act):
            act.wait_ge(eps_made, 1)
            nc.scalar.activation(std[:, 0:1], eps[0:LP, :], ACT.Sqrt).then_inc(table_loaded, 1)
            act.wait_ge(table_loaded, 1)

            def deviations(k):
                at = slice(NORM_CUTS[k], NORM_CUTS[k + 1])
                act.wait_ge(aggr_done, k + 1)
                nc.scalar.activation(std[:, at], mv[:, at, 1], ACT.Sqrt, bias=eps[0:LP, :]).then_inc(std_ready, 1)

            def tile_deviations(q):
                at = slice(q * GT, (q + 1) * GT)
                act.wait_ge(t_aggr_done, q + 1)
                nc.scalar.activation(t_std[:, at], t_mv[:, at, 1], ACT.Sqrt, bias=eps[:, :]).then_inc(t_std_ready, 1)

            deviations(0)
            for k in range(NORM_STEPS):
                if k + 1 < NORM_STEPS:
                    deviations(k + 1)
                else:
                    tile_deviations(0)
                act.wait_ge(norm_ready, k + 1)
                for c in range(NORM_CUTS[k], NORM_CUTS[k + 1]):
                    nc.scalar.activation(h_all[0:LP, c, :], x_all[0:LP, c, :], ACT.Relu, bias=nmr[:, c:c + 1],
                                         scale=rstd[:, c:c + 1]).then_inc(h_ready, 1)

            act.wait_ge(src0_i, 1)

            def tile_h(q):
                act.wait_ge(t_norm_ready, q + 1)
                for t in range(q * GT, (q + 1) * GT):
                    nc.scalar.activation(hg[:, t, :], hg[:, t, :], ACT.Relu, bias=t_nmr[:, t:t + 1],
                                         scale=t_rstd[:, t:t + 1]).then_inc(t_h_ready, 1)

            def stage(g, q):
                act.wait_ge(group_summed, g + 1)
                settled(act)
                nc.scalar.activation(idx[:, q * GT:(q + 1) * GT], src_i[:, bass.ds((g + GROUPS) * GT, GT)],
                                     ACT.Copy).then_inc(idx_ready, 1)

            def own(b):
                if static(b):
                    act.wait_ge(h_blocks_in, 16 * (LOADS + 1))
                else:
                    act.wait_ge(block_T, b)
                settled(act)
                nc.scalar.activation(h_own[0:BLK, :], h_all[0:BLK, bass.ds(b, 1), :].rearrange("p a f -> p (a f)"),
                                     ACT.Copy).then_inc(own_h, 1)

            def slot_of(b):
                return bass.ds((b % RING) * SEG, SEG)

            def take(b, slot):
                act.wait_ge(summed, b + 1)
                if not static(b):
                    act.wait_ge(block_T, b)
                settled(act)
                nc.scalar.activation(cnt_row[:, :], ring[0:1, 1, slot], ACT.Copy).then_inc(taken, 1)
                if not static(b):
                    act.wait_ge(z_high, b)
                settled(act)
                nc.scalar.activation(blk[:, :, :], ring[:, 0, slot].rearrange("p (n r) -> p r n", r=R),
                                     ACT.Copy).then_inc(taken, 1)

            def clear(b, slot, a):
                act.wait_ge(taken, 2 * (b + 1))
                settled(act)
                nc.scalar.activation(ring[:, a, slot], zeros[:, :], ACT.Copy).then_inc(slot_clear, 1)

            def block_copies(b):
                act.wait_ge(block_T, b + 1)
                if not static(b):
                    act.wait_ge(z_root, b)
                nc.scalar.activation(hT[:, :], zp[:, 0:BLK], ACT.Copy).then_inc(block_sb, 1)
                if not static(b):
                    act.wait_ge(inv_step, INV_STEPS * b)
                nc.scalar.activation(cnt[:, :], cntT, ACT.Copy).then_inc(block_sb, 1)

            def iteration(i):
                b = block_of(i, LAG)
                slot = slot_of(b) if b is not None else None
                for q in range(GROUPS):
                    if static(i):
                        if q + 1 < GROUPS:
                            tile_deviations(q + 1)
                        tile_h(q)
                    g = i * GROUPS + q - 1
                    if not static(g, -1) and not (isinstance(g, int) and g + GROUPS >= GALL):
                        stage(g, (q - 1) % GROUPS)
                    if b is not None:
                        if q == 1:
                            own(b)
                        if q == 2:
                            take(b, slot)
                        if q == 3:
                            block_copies(b)
                        if q >= 3:
                            clear(b, slot, q - 3)

            def end():
                for b in LASTB:
                    own(b)
                    take(b, slot_of(b))
                    block_copies(b)

            def other_sources():
                act.wait_ge(srcs_T, 1)
                nc.scalar.activation(src_i[:, P:], srcT, ACT.Copy).then_inc(srcs_i, 1)
                act.wait_ge(zeros_made, 1)
                act.wait_ge(srcs_i, 1)

            run_iterations(act, iteration, end, other_sources)

            act.wait_ge(flag_ready, 1)
            general = act.value_load(flag[0:1, 0:1], min_val=0, max_val=1)
            with act.If(general):
                def block_h(b, n):
                    if not static(b):
                        act.wait_ge(g_y, b)
                        settled(act)
                    nc.scalar.activation(h_own[0:BLK, :], h_all[0:BLK, bass.ds(b, 1), :].rearrange("p a f -> p (a f)"),
                                         ACT.Copy).then_inc(g_own, 1)
                    act.wait_ge(g_own_T, b + 1)
                    nc.scalar.activation(hT[:, 0:n], zp[:, 0:n], ACT.Copy).then_inc(g_own_sb, 1)
                    act.wait_ge(g_T, b + 1)
                    settled(act)
                    for r in range(R):
                        at = (r % (R // 2)) * BLK
                        nc.scalar.activation(blk[:, r, 0:n], fin[:, r // (R // 2), at:at + n], ACT.Copy).then_inc(g_means_sb, 1)

                block_h(0, BLK)
                with act.Fori(1, BLOCKS - 1) as b:
                    block_h(b, BLK)
                block_h(BLOCKS - 1, LASTN)

        @block.vector
        def _(dve):
            nc.vector.memset(eps[:, :], EPS).then_inc(eps_made, 1)
            dve.wait_ge(src0_in, 16)
            nc.vector.tensor_copy(e_rows[:, 0, 0, :], e_rows_i[:, 0, 0, :]).then_inc(src0_f, 1)
            dve.wait_ge(src0_T, 1)
            nc.vector.tensor_copy(idx[:, :], zp[:, 0:IT]).then_inc(idx_ready, GROUPS)
            nc.vector.tensor_copy(src_i[:, 0:P], zp[:, 0:P]).then_inc(src0_i, 1)

            def moments(k):
                dve.wait_ge(x_in[k], 16)
                for c in range(NORM_CUTS[k], NORM_CUTS[k + 1]):
                    last = nc.vector.bn_stats(stats[:, c, :], x_all[0:LP, c, :])
                last.then_inc(stats_done, 1)
                if k:
                    scales(k - 1)
                dve.wait_ge(stats_done, k + 1)
                for c in range(NORM_CUTS[k], NORM_CUTS[k + 1]):
                    last = nc.vector.bn_aggr(mv[:, c, :], stats[:, c, :])
                last.then_inc(aggr_done, 1)

            def scales(k):
                at = slice(NORM_CUTS[k], NORM_CUTS[k + 1])
                dve.wait_ge(std_ready, k + 1)
                nc.vector.reciprocal(rstd[:, at], std[:, at]).then_inc(rstd_done, 1)
                dve.wait_ge(rstd_done, k + 1)
                nc.vector.scalar_tensor_tensor(out=nmr[:, at], in0=mv[:, at, 0], scalar=-1.0,
                                               in1=rstd[:, at], op0=ALU.mult, op1=ALU.mult).then_inc(norm_ready, 1)

            def tile_moments(q):
                for t in range(q * GT, (q + 1) * GT):
                    dve.wait_ge(gathered[t], 16)
                    last = nc.vector.bn_stats(t_stats[:, t, :], hg[:, t, :])
                last.then_inc(t_stats_done, 1)
                dve.wait_ge(t_stats_done, q + 1)
                for t in range(q * GT, (q + 1) * GT):
                    last = nc.vector.bn_aggr(t_mv[:, t, :], t_stats[:, t, :])
                last.then_inc(t_aggr_done, 1)

            def tile_scales(q):
                at = slice(q * GT, (q + 1) * GT)
                dve.wait_ge(t_std_ready, q + 1)
                nc.vector.reciprocal(t_rstd[:, at], t_std[:, at]).then_inc(t_rstd_done, 1)
                dve.wait_ge(t_rstd_done, q + 1)
                nc.vector.scalar_tensor_tensor(out=t_nmr[:, at], in0=t_mv[:, at, 0], scalar=-1.0,
                                               in1=t_rstd[:, at], op0=ALU.mult, op1=ALU.mult).then_inc(t_norm_ready, 1)

            for k in range(NORM_STEPS):
                moments(k)
                if k == 5:
                    dve.wait_ge(edges_in[2], 64)
                    nc.vector.tensor_copy(e_rows[:, 2, :, :], e_rows_i[:, 2, :, :]).then_inc(type_conv, 1)
                if k == 6:
                    dve.wait_ge(dst_T, 1)
                    nc.vector.tensor_copy(dst_f[:, :], dstT).then_inc(dst_sb, 1)
            tile_moments(0)
            dve.wait_ge(type_T, 1)
            nc.vector.scalar_tensor_tensor(out=seg_f[:, :], in0=dst_f[:, :], scalar=float(R), in1=typeT,
                                           op0=ALU.mult, op1=ALU.add).then_inc(seg_ready, 1)
            scales(NORM_STEPS - 1)
            dve.wait_ge(base_T, 1)
            nc.vector.tensor_scalar(base8[:, :], baseT, float(R), None, ALU.mult).then_inc(base_ready, 1)
            dve.wait_ge(seg_ready, 1)
            dve.wait_ge(base_ready, 1)
            rels = rel_f[:, :].rearrange("p (g j) -> p g j", j=GT)
            nc.vector.tensor_tensor(rels, seg_f[:, 0:TILES].rearrange("p (g j) -> p g j", j=GT),
                                    base8[:, :].unsqueeze(2).to_broadcast([P, GALL, GT]),
                                    ALU.subtract).then_inc(rel_ready, 1)
            tile_moments(1)
            tile_scales(0)
            dve.wait_ge(iota_made, 1)
            dve.wait_ge(rel_ready, 1)

            def windows_in_ring():
                dve.wait_ge(low_made, 1)
                nc.vector.tensor_tensor(dev8[:, :], base8[:, :], low8[:, 0:GALL], ALU.subtract).then_inc(near_step, 1)
                dve.wait_ge(near_step, 1)
                nc.vector.tensor_scalar(near8[:, :], dev8[:, :], 0.0, float(LIVE * SEG - WIN), ALU.max,
                                        ALU.min).then_inc(near_step, 1)
                dve.wait_ge(near_step, 2)
                nc.vector.tensor_scalar(near8[:, ENDG:], near8[:, ENDG:], float(SEG), None, ALU.max).then_inc(near_step, 1)
                dve.wait_ge(near_step, 3)
                nc.vector.tensor_tensor(near8[:, :], near8[:, :], low8[:, 0:GALL], ALU.add).then_inc(near_step, 1)
                dve.wait_ge(laps_made, 1)
                dve.wait_ge(near_step, 4)
                nc.vector.tensor_scalar(laps[:, :], near8[:, :], laps_at[:, 0:1], None, ALU.is_ge).then_inc(laps_ready, 1)

            def places():
                dve.wait_ge(laps_T, 1)
                nc.vector.scalar_tensor_tensor(out=at_i[:, :], in0=lapsT, scalar=-float(SPAN), in1=near8[0:1, :],
                                               op0=ALU.mult, op1=ALU.add).then_inc(at_ready, 1)
                dve.wait_ge(at_ready, 1)
                dve.wait_ge(ring_cleared, 1)

            def onehots(i, q, n, between):
                g = i * GROUPS + q
                if not static(i):
                    dve.wait_ge(group_summed, g - GROUPS + 1)
                for j in range(n):
                    t = q * GT + j
                    a, e = WINDOWS[j]
                    nc.vector.tensor_scalar(onehot[:, t, 0:(e - a) * R], iota[:, a * R:e * R],
                                            rel_f[:, bass.ds(i * IT + t, 1)], None,
                                            ALU.is_equal).then_inc(onehot_ready, 1)
                    if between:
                        between.pop(0)()

            def add_group(g, q, n, cleared_slots):
                start = dve.value_load(at_i[0:1, bass.ds(g, 1)], min_val=0, max_val=SPAN - R)
                width = WINDOWS[n - 1][1] * R
                at = bass.ds(start, width)
                if cleared_slots is not None:
                    dve.wait_ge(slot_clear, cleared_slots)
                if not static(g):
                    dve.wait_ge(group_added, g)
                dve.wait_ge(group_summed, g + 1)
                nc.vector.tensor_tensor(ring[:, :, at], ring[:, :, at], acc[:, q, :, 0:width],
                                        ALU.add).then_inc(group_added, 1)

            def finish_sums(b, groups):
                dve.wait_ge(group_added, groups)

                def fold():
                    k = b // RING
                    nc.vector.tensor_tensor(ring[:, :, 0:WIN], ring[:, :, 0:WIN], ring[:, :, SPAN:],
                                            ALU.add).then_inc(fold_done, 1)
                    dve.wait_ge(fold_done, 2 * k + 1)
                    if isinstance(b, int) and b + RING >= BLOCKS:
                        return
                    nc.vector.memset(ring[:, :, SPAN:], 0.0).then_inc(fold_done, 1)
                    dve.wait_ge(fold_done, 2 * k + 2)
                    settled(dve)

                if not isinstance(b, int):
                    with dve.If((b % RING) == 0):
                        fold()
                elif b % RING == 0:
                    fold()
                dve.sem_inc(summed, 1)

            def inverse_counts(b):
                def at_least_one():
                    dve.wait_ge(block_sb, 2 * (b + 1))
                    nc.vector.tensor_scalar(cnt1[:, :], cnt[:, :], 1.0, None, ALU.max).then_inc(inv_step, 1)

                def inverse():
                    if not static(b):
                        dve.wait_ge(y_ready, b)
                    dve.wait_ge(inv_step, INV_STEPS * b + 1)
                    settled(dve)
                    nc.vector.reciprocal(inv[:, :], cnt1[:, :]).then_inc(inv_step, 1)

                return [at_least_one, inverse]

            def add_terms(b, terms):
                x_b = x_all[0:BLK, bass.ds(b, 1), :].rearrange("p a f -> p (a f)")

                def term(k):
                    def step():
                        done = y_ready if k == ADDS - 1 else term_added
                        if k == 0:
                            if static(b):
                                dve.wait_ge(x_blocks_in, 16 * (LOADS + 1))
                            dve.wait_ge(z_root, b + 1)
                            nc.vector.tensor_tensor(x_b, zp[0:BLK, 0:F], x_b, ALU.add).then_inc(done, 1)
                            return
                        r = k - 1
                        if r == 0:
                            dve.wait_ge(z_low, b + 1)
                            dve.wait_ge(inv_step, INV_STEPS * (b + 1))
                        if r == R // 2:
                            dve.wait_ge(z_high, b + 1)
                        dve.wait_ge(term_added, terms_before(b) + k)
                        at = (r % (R // 2)) * F
                        nc.vector.scalar_tensor_tensor(out=x_b, in0=fin[0:BLK, r // (R // 2), at:at + F],
                                                       scalar=inv[:, r:r + 1], in1=x_b,
                                                       op0=ALU.mult, op1=ALU.add).then_inc(done, 1)
                    return step

                return [term(k) for k in terms]

            def iteration(i):
                b, done = block_of(i, LAG), block_of(i, LAG + 1)
                for q in range(GROUPS):
                    g = i * GROUPS + q
                    between = []
                    if done is not None:
                        if q == 1:
                            between = inverse_counts(done)
                        if q >= 2:
                            between = add_terms(done, range((q - 2) * 3, (q - 1) * 3))
                    if tiles_in(i, q):
                        onehots(i, q, tiles_in(i, q), between)
                    for step in between:
                        step()
                    if static(i):
                        if q + 2 < GROUPS:
                            tile_moments(q + 2)
                        if q + 1 < GROUPS:
                            tile_scales(q + 1)
                        if q == 0:
                            windows_in_ring()
                        if q == 1:
                            places()
                    if not (isinstance(g, int) and (g < 2 or g - 2 >= GALL)):
                        at = (i - 1, q + 3) if q < 2 else (i, q - 2)
                        add_group(g - 2, at[1], tiles_in(*at), 2 * (done + 1) if q == 2 and done is not None else None)
                    if q == 1 and b is not None:
                        finish_sums(b, min(i * GROUPS, GALL) if isinstance(i, int) else i * GROUPS)

            def check_order():
                dve.wait_ge(edges_in[0], 48)
                nc.vector.tensor_copy(e_rows[:, 0, 1:CHUNKS, :], e_rows_i[:, 0, 1:CHUNKS, :]).then_inc(srcs_conv, 1)
                cols = []

                def extreme(values, p, op, limit, neutral=None):
                    c = len(cols)
                    if neutral is not None:
                        nc.vector.memset(ext[:, c:c + 1], neutral).then_inc(check_step, 1)
                        steps[0] += 1
                        dve.wait_ge(check_step, steps[0])
                    nc.vector.tensor_reduce(ext[0:p, c:c + 1], values, AX.X, op).then_inc(check_step, 1)
                    steps[0] += 1
                    cols.append((limit, ALU.is_gt if op == ALU.max else ALU.is_lt))

                steps = [0]
                for j, (a, e) in enumerate(WINDOWS):
                    groups = GALL - (j == GT - 1)
                    for op, limit in ((ALU.max, e * R - 0.5), (ALU.min, a * R - 0.5)):
                        extreme(rels[:, 0:groups, j], P, op, limit)
                a, e = WINDOWS[GT - 1]
                for op, limit in ((ALU.max, e * R - 0.5), (ALU.min, a * R - 0.5)):
                    extreme(rel_f[0:EDGES_L, TILES - 1:TILES], EDGES_L, op, limit, float(a * R))
                for op, limit in ((ALU.max, LIVE * SEG - WIN + 0.5), (ALU.min, -0.5)):
                    extreme(dev8[:, :], P, op, limit)
                extreme(dev8[:, ENDG:], P, ALU.min, SEG - 0.5)
                dve.wait_ge(check_step, steps[0])
                for c, (limit, cmp) in enumerate(cols):
                    last = nc.vector.tensor_scalar(bad[:, c:c + 1], ext[:, c:c + 1], limit, None, cmp)
                last.then_inc(check_step, 1)
                steps[0] += 1
                dve.wait_ge(check_step, steps[0])
                assert len(cols) == CHECKS
                nc.vector.tensor_reduce(bad1[:, :], bad[:, :], AX.X, ALU.max).then_inc(bad_ready, 1)
                dve.wait_ge(bad_sum, 1)
                nc.vector.tensor_scalar(flag[:, :], zp[0:1, 0:1], 1.0, None, ALU.min).then_inc(flag_ready, 1)

            def in_turn(steps):
                for step in steps:
                    step()

            def add_last_terms(b):
                x_b = x_all[0:BLK, b, :]
                dve.wait_ge(z_root, b + 1)
                nc.vector.tensor_tensor(x_b, zp[0:BLK, 0:F], x_b, ALU.add).then_inc(term_added, 1)
                dve.wait_ge(z_low, b + 1)
                dve.wait_ge(inv_step, INV_STEPS * (b + 1))
                for r in range(R):
                    z = fin[0:BLK, r // (R // 2), (r % (R // 2)) * F:(r % (R // 2) + 1) * F]
                    if r == R // 2:
                        dve.wait_ge(z_high, b + 1)
                    if r == 0:
                        dve.wait_ge(y_ready, b)
                        nc.vector.tensor_scalar(even[:, :], z, inv[:, r:r + 1], None, ALU.mult).then_inc(term_added, 1)
                    else:
                        to = x_b if r % 2 else even[:, :]
                        dve.wait_ge(term_added, terms_before(b) + r)
                        nc.vector.scalar_tensor_tensor(out=to, in0=z, scalar=inv[:, r:r + 1], in1=to,
                                                       op0=ALU.mult, op1=ALU.add).then_inc(term_added, 1)
                dve.wait_ge(term_added, terms_before(b + 1))
                nc.vector.tensor_tensor(x_b, even[:, :], x_b, ALU.add).then_inc(y_ready, 1)

            def end():
                b1, b2, b3 = LASTB
                for q in range(2):
                    onehots(ITERS - 1, q, tiles_in(ITERS - 1, q), [])
                for g in (ENDG - 2, ENDG - 1):
                    add_group(g, g % GROUPS, GT, None)
                finish_sums(b1, ENDG)
                finish_sums(b2, ENDG)
                in_turn(inverse_counts(ENDB))
                add_last_terms(ENDB)
                in_turn(inverse_counts(b1))
                add_group(ENDG, 0, GT, 2 * (ENDB + 1))
                add_group(ENDG + 1, 1, GT, None)
                finish_sums(b3, GALL)
                add_last_terms(b1)
                for b in (b2, b3):
                    in_turn(inverse_counts(b))
                    add_last_terms(b)

            run_iterations(dve, iteration, end, check_order)

            dve.wait_ge(flag_ready, 1)
            general = dve.value_load(flag[0:1, 0:1], min_val=0, max_val=1)
            with dve.If(general):
                def chained(ins, k):
                    ins.then_inc(g_step, 1)
                    dve.wait_ge(g_step, k)
                    settled(dve)

                chained(nc.vector.memset(g_h[:, F:VW], 0.0), 1)
                chained(nc.vector.memset(g_h[:, F:F + 1], 1.0), 2)
                dve.wait_ge(g_const, 3)

                TILE_STEPS = 5
                def edge_tile(t):
                    s0 = 2 + t * TILE_STEPS
                    if not static(t):
                        dve.wait_ge(g_added, 16 * t)
                        settled(dve)
                    nc.vector.tensor_copy(g_idx[:, :], src_i[:, bass.ds(t, 1)]).then_inc(g_idx_ready, 1)
                    key = seg_f[:, bass.ds(t, 1)]
                    nc.vector.tensor_scalar(g_key[:, :], ones[:, :], key, None, ALU.mult).then_inc(g_keys, 1)
                    dve.wait_ge(g_spread, t + 1)
                    nc.vector.tensor_scalar(g_eq[:, :], fin[:, 0, 0:P], key, None, ALU.is_equal).then_inc(g_eq_ready, 1)
                    dve.wait_ge(g_eq_ready, t + 1)
                    chained(nc.vector.tensor_tensor(g_before[:, :], g_eq[:, :], g_low[:, :], ALU.mult), s0 + 1)
                    chained(nc.vector.tensor_reduce(g_col[:, 0:1], g_before[:, :], AX.X, ALU.add), s0 + 2)
                    chained(nc.vector.tensor_scalar(g_col[:, 0:1], g_col[:, 0:1], 0.5, None, ALU.is_lt), s0 + 3)
                    chained(nc.vector.scalar_tensor_tensor(out=g_col[:, 1:2], in0=key, scalar=-0.5, in1=g_col[:, 0:1],
                                                           op0=ALU.is_gt, op1=ALU.mult), s0 + 4)
                    chained(nc.vector.tensor_tensor(g_col[:, 2:3], key, g_row[:, :], ALU.subtract), s0 + 5)
                    nc.vector.scalar_tensor_tensor(out=g_put[:, :], in0=g_col[:, 1:2], scalar=g_col[:, 2:3],
                                                   in1=g_row[:, :], op0=ALU.mult, op1=ALU.add).then_inc(g_put_written, 1)
                    dve.wait_ge(g_put_written, t + 1)
                    dve.wait_ge(g_summed, t + 1)
                    settled(dve)
                    nc.vector.tensor_copy(g_v[:, :], fin[:, 1, 0:VW]).then_inc(g_put_ready, 1)

                edge_tile(0)
                with dve.Fori(1, TILES) as t:
                    edge_tile(t)

                def block_means(b, n, first_step):
                    dve.wait_ge(g_in, 16 * (b + 1))
                    dve.wait_ge(g_sums_in, 16 * (b + 1))
                    settled(dve)
                    chained(nc.vector.tensor_scalar(g_c[0:n, :], g_s[0:n, :, F], 1.0, None, ALU.max), first_step + 1)
                    chained(nc.vector.reciprocal(g_c[0:n, :], g_c[0:n, :]), first_step + 2)
                    for r in range(R):
                        last = nc.vector.tensor_scalar(g_s[0:n, r, 0:F], g_s[0:n, r, 0:F], g_c[0:n, r:r + 1], None, ALU.mult)
                    last.then_inc(g_means, 1)
                    dve.wait_ge(g_z, b + 1)
                    settled(dve)
                    nc.vector.tensor_tensor(g_out[0:n, :], zp[0:n, 0:F], g_x[0:n, :], ALU.add).then_inc(g_y, 1)

                steps_before = 2 + TILES * TILE_STEPS
                with dve.Fori(0, BLOCKS - 1) as b:
                    block_means(b, BLK, steps_before + 2 * b)
                block_means(BLOCKS - 1, LASTN, steps_before + 2 * (BLOCKS - 1))

        @block.tensor
        def _(pe):
            pe.wait_ge(ident_made, 2)
            pe.wait_ge(src0_f, 1)
            nc.tensor.transpose(zp[:, 0:P], e_rows[:, 0, 0, :], ident[:, :]).then_inc(src0_T, 1)

            def transposes(to, a, c0, done):
                for c in range(c0, CHUNKS):
                    last = nc.tensor.transpose(to[:, (c - c0) * P:(c - c0 + 1) * P], e_rows[:, a, c, :], ident[:, :])
                last.then_inc(done, 1)

            pe.wait_ge(dst_conv, 1)
            transposes(dstT, 1, 0, dst_T)
            pe.wait_ge(dst_sb, 1)
            pe.wait_ge(first_made, 1)
            nc.tensor.matmul(baseT, first[:, :], dst_f[:, 0:TILES].rearrange("p (g j) -> p g j", j=GT)[:, :, 0],
                             start=True, stop=True).then_inc(base_T, 1)
            pe.wait_ge(type_conv, 1)
            transposes(typeT, 2, 0, type_T)
            pe.wait_ge(src0_i, 1)
            pe.wait_ge(seg_ready, 1)
            pe.wait_ge(base_ready, 1)

            def count_laps():
                pe.wait_ge(laps_ready, 1)
                pe.wait_ge(ones_made, 2)
                nc.tensor.matmul(lapsT, ones[:, 0:1], laps[:, :], start=True, stop=True).then_inc(laps_T, 1)

            def sums_of(i, q, n):
                g = i * GROUPS + q
                if not static(i):
                    pe.wait_ge(group_added, g - GROUPS + 1)
                for j in range(n):
                    t = q * GT + j
                    a, e = WINDOWS[j]
                    at, width = slice(a * R, e * R), (e - a) * R
                    pe.wait_ge(onehot_ready, i * IT + t + 1)
                    if static(i):
                        pe.wait_ge(t_h_ready, t + 1)
                    else:
                        pe.wait_ge(gathered[t], 16 * (i + 1))
                    nc.tensor.matmul(acc[:, q, 0, at], hg[:, t, :], onehot[:, t, 0:width],
                                     start=(j == 0), stop=(j == n - 1), skip_group_check=True)
                    halves = onehot[:, t, 0:width].bitcast(bf16).rearrange("p (w h) -> p w h", h=2)[:, :, 1]
                    last = nc.tensor.matmul(acc[:, q, 1, at], ones_bf[:, :], halves,
                                            start=False, stop=(j == n - 1), skip_group_check=True)
                last.then_inc(group_summed, 1)

            def block_transposes(b):
                pe.wait_ge(own_h, b + 1)
                if not static(b):
                    pe.wait_ge(term_added, terms_before(b - 1) + 1)
                nc.tensor.transpose(zp[:, 0:BLK], h_own[0:BLK, :], ident[0:BLK, 0:BLK])
                pe.wait_ge(taken, 2 * b + 1)
                settled(pe)
                counts = cnt_row[:, :].rearrange("p (n r) -> p n r", r=R)
                for r in range(R):
                    last = nc.tensor.transpose(cntT[:, r:r + 1], counts[:, :, r], ident[0:1, 0:1])
                last.then_inc(block_T, 1)

            def relations(b, r0, r1, done):
                if r0 == 0:
                    pe.wait_ge(taken, 2 * (b + 1))
                if not static(b) and r0 % (R // 2) == 0:
                    if r0 == 0:
                        pe.wait_ge(term_added, terms_before(b - 1) + R // 2 + 1)
                    else:
                        pe.wait_ge(y_ready, b)
                for r in range(r0, r1):
                    at = (r % (R // 2)) * F
                    last = nc.tensor.matmul(fin[0:BLK, r // (R // 2), at:at + F], blk[:, r, :], w_sb[:, r, :],
                                            start=True, stop=True)
                if done is not None:
                    last.then_inc(done, 1)

            def root(n, first_one):
                nc.tensor.matmul(zp[0:n, 0:F], hT[:, 0:n], wr_sb[:, :], start=first_one, stop=False)
                return nc.tensor.matmul(zp[0:n, 0:F], ones[0:1, 0:n], bias_sb[:, :], start=False, stop=True)

            def root_of(b):
                pe.wait_ge(block_sb, 2 * (b + 1))
                root(BLK, True).then_inc(z_root, 1)

            def iteration(i):
                b, done = block_of(i, LAG), block_of(i, LAG + 1)
                for q in range(GROUPS):
                    n = tiles_in(i, q)
                    if n:
                        sums_of(i, q, n)
                    if static(i) and q == 0:
                        count_laps()
                    if q == 0 and done is not None:
                        relations(done, R // 2, R, z_high)
                    if b is not None:
                        if q == 2:
                            block_transposes(b)
                        if q == 3:
                            relations(b, 0, R // 2 - 1, None)
                        if q == 4:
                            relations(b, R // 2 - 1, R // 2, z_low)
                            root_of(b)

            def check_sum():
                pe.wait_ge(srcs_conv, 1)
                transposes(srcT, 0, 1, srcs_T)
                pe.wait_ge(at_ready, 1)
                pe.wait_ge(bad_ready, 1)
                nc.tensor.matmul(zp[0:1, 0:1], bad1[:, :], ones[:, 0:1], start=True, stop=True).then_inc(bad_sum, 1)
                pe.wait_ge(srcs_i, 1)
                pe.wait_ge(flag_ready, 1)
                pe.wait_ge(consts_in, 48)

            def end():
                b1, b2, b3 = LASTB
                relations(ENDB, R // 2, R, z_high)
                sums_of(ITERS - 1, 0, GT)
                block_transposes(b1)
                sums_of(ITERS - 1, 1, GT)
                for b in LASTB:
                    if b != b1:
                        block_transposes(b)
                    relations(b, 0, R // 2, z_low)
                    root_of(b)
                    relations(b, R // 2, R, z_high)

            run_iterations(pe, iteration, end, check_sum)

            general = pe.value_load(flag[0:1, 0:1], min_val=0, max_val=1)
            with pe.If(general):
                with pe.Fori(0, TILES) as t:
                    pe.wait_ge(g_keys, t + 1)
                    nc.tensor.matmul(fin[:, 0, 0:P], g_key[:, :], ident[:, :], start=True, stop=True).then_inc(g_spread, 1)
                    pe.wait_ge(g_eq_ready, t + 1)
                    pe.wait_ge(g_gathered, 16 * (t + 1))
                    nc.tensor.matmul(fin[:, 1, 0:VW], g_eq[:, :], g_h[:, :], start=True, stop=True).then_inc(g_summed, 1)

                def block_out(b, n):
                    pe.wait_ge(g_own, b + 1)
                    nc.tensor.transpose(zp[:, 0:n], h_own[0:n, :], ident[0:n, 0:n]).then_inc(g_own_T, 1)
                    pe.wait_ge(g_means, b + 1)
                    for r in range(R):
                        at = (r % (R // 2)) * BLK
                        last = nc.tensor.transpose(fin[:, r // (R // 2), at:at + n], g_s[0:n, r, 0:F], ident[0:n, 0:n])
                    last.then_inc(g_T, 1)
                    pe.wait_ge(g_own_sb, b + 1)
                    pe.wait_ge(g_means_sb, R * (b + 1))
                    for r in range(R):
                        nc.tensor.matmul(zp[0:n, 0:F], blk[:, r, 0:n], w_sb[:, r, :], start=(r == 0), stop=False)
                    root(n, False).then_inc(g_z, 1)

                with pe.Fori(0, BLOCKS - 1) as b:
                    block_out(b, BLK)
                block_out(BLOCKS - 1, LASTN)


_INS = ["x", "src", "dst", "edge_type_8", "L0_gnn_W", "L0_gnn_W_root", "L0_gnn_bias"]


def kernel(**inputs):
    import concourse.bacc as bacc
    from concourse.bass_utils import run_bass_kernel_spmd as run

    nc = bacc.Bacc("TRN2", target_bir_lowering=False, num_devices=1)
    arrays, args = {}, []
    for name in _INS:
        a = np.ascontiguousarray(inputs[name])
        arrays[f"in_{name}"] = a
        args.append(nc.dram_tensor(f"in_{name}", a.shape, mybir.dt.from_np(a.dtype), kind="ExternalInput").ap())
    out = nc.dram_tensor("out_0", (N, F), mybir.dt.float32, kind="ExternalOutput").ap()
    rgcn(nc, *args, out)
    r = run(nc, [arrays], core_ids=[0])
    return r.results[0]["out_0"]
```
